# Optimizing a Trainium2 kernel written in Bass

```python
import numpy as np
import jax
import jax.numpy as jnp

def _softmax(x, axis=-1):
    return jax.nn.softmax(x, axis=axis)

def _gelu(x):
    return jax.nn.gelu(x, approximate=True)

def _silu(x):
    return jax.nn.silu(x)

def _sigmoid(x):
    return jax.nn.sigmoid(x)

def _layernorm(x, axis=-1, eps=1e-05):
    m = jnp.mean(x, axis=axis, keepdims=True)
    v = jnp.var(x, axis=axis, keepdims=True)
    return (x - m) / jnp.sqrt(v + eps)

def _scatter_add(tgt, idx, src, axis=0):
    return tgt.at[idx].add(src)

def _segment_sum(src, seg, n):
    return jax.ops.segment_sum(src, seg, n)
kernel_name = 'mk_hybrid_d1_jaxref_r8_c9af60'

def setup_inputs(seed: int=0):
    np.random.seed(seed)
    _w = jnp.asarray

    def _L0_attn_a_setup():
        import jax, jax.numpy as jnp
        import numpy as np
        D_MODEL = 128
        EXPAND = 2
        D_INNER = EXPAND * D_MODEL
        HEADDIM = 64
        NHEADS = D_INNER // HEADDIM
        D_STATE = 64
        D_CONV = 4
        BATCH = 2
        SEQ_LEN = 128
        LN_EPS = 1e-05

        def _layernorm(x, w, b):
            mu = jnp.mean(x, axis=-1, keepdims=True)
            var = jnp.var(x, axis=-1, keepdims=True)
            return (x - mu) * jax.lax.rsqrt(var + LN_EPS) * w + b

        def _forward(hidden_states, in_proj_w, conv_w, conv_b, A_log, dt_w, dt_b, B_w, C_w, D, ln_w, ln_b, out_proj_w):
            B_, L, _ = hidden_states.shape
            xz = hidden_states @ in_proj_w.T
            x, z = jnp.split(xz, 2, axis=-1)
            x_ncl = jnp.transpose(x, (0, 2, 1))
            x_conv = jax.lax.conv_general_dilated(x_ncl, conv_w, window_strides=(1,), padding=[(D_CONV - 1, 0)], dimension_numbers=('NCH', 'OIH', 'NCH'), feature_group_count=D_INNER)
            x_conv = x_conv + conv_b[None, :, None]
            x = jnp.transpose(x_conv, (0, 2, 1))
            x = jax.nn.silu(x)
            dt = jax.nn.softplus(x @ dt_w.T + dt_b)
            Bm = (x @ B_w.T).reshape(B_, L, NHEADS, D_STATE)
            Cm = (x @ C_w.T).reshape(B_, L, NHEADS, D_STATE)
            xh = x.reshape(B_, L, NHEADS, HEADDIM)
            A = -jnp.exp(A_log)
            h0 = jnp.zeros((B_, NHEADS, HEADDIM, D_STATE), x.dtype)

            def step(h, inp):
                x_t, dt_t, B_t, C_t = inp
                A_bar = jnp.exp(A[None, :] * dt_t)[..., None, None]
                h = A_bar * h + dt_t[..., None, None] * B_t[:, :, None, :] * x_t[..., None]
                y_t = jnp.einsum('bhpn,bhn->bhp', h, C_t) + D[None, :, None] * x_t
                return (h, y_t)
            xs = (jnp.transpose(xh, (1, 0, 2, 3)), jnp.transpose(dt, (1, 0, 2)), jnp.transpose(Bm, (1, 0, 2, 3)), jnp.transpose(Cm, (1, 0, 2, 3)))
            h_final, y = jax.lax.scan(step, h0, xs)
            y = jnp.transpose(y, (1, 0, 2, 3)).reshape(B_, L, D_INNER)
            y = _layernorm(y, ln_w, ln_b)
            y = y * jax.nn.silu(z)
            output = y @ out_proj_w.T
            return (output, h_final)

        def _reference_tuple_inner(hidden_states, in_proj_w, conv_w, conv_b, A_log, dt_w, dt_b, B_w, C_w, D, ln_w, ln_b, out_proj_w):
            return _forward(hidden_states, in_proj_w, conv_w, conv_b, A_log, dt_w, dt_b, B_w, C_w, D, ln_w, ln_b, out_proj_w)
        key = jax.random.key(seed)
        ks = jax.random.split(key, 12)
        s = 0.02
        return {'hidden_states': jax.random.normal(ks[0], (BATCH, SEQ_LEN, D_MODEL), jnp.float32), 'in_proj_w': jax.random.normal(ks[1], (2 * D_INNER, D_MODEL), jnp.float32) * s, 'conv_w': jax.random.normal(ks[2], (D_INNER, 1, D_CONV), jnp.float32) * 0.1, 'conv_b': jax.random.normal(ks[3], (D_INNER,), jnp.float32) * 0.01, 'A_log': jnp.zeros((NHEADS,), jnp.float32), 'dt_w': jax.random.normal(ks[4], (NHEADS, D_INNER), jnp.float32) * s, 'dt_b': jax.random.normal(ks[5], (NHEADS,), jnp.float32) * 0.1, 'B_w': jax.random.normal(ks[6], (NHEADS * D_STATE, D_INNER), jnp.float32) * s, 'C_w': jax.random.normal(ks[7], (NHEADS * D_STATE, D_INNER), jnp.float32) * s, 'D': jnp.ones((NHEADS,), jnp.float32), 'ln_w': jnp.ones((D_INNER,), jnp.float32), 'ln_b': jnp.zeros((D_INNER,), jnp.float32), 'out_proj_w': jax.random.normal(ks[8], (D_MODEL, D_INNER), jnp.float32) * s}
    _L0_attn_a_in = _L0_attn_a_setup()

    def _L0_attn_b_setup():
        import jax, jax.numpy as jnp
        import numpy as np
        B, T, D = (2, 256, 128)
        H = 16
        HD = D // H
        DL = 64
        NR = 64
        EPS = 1.1920929e-07

        def _rms_norm(x, w):
            ms = jnp.mean(jnp.square(x), axis=-1, keepdims=True)
            return x * jax.lax.rsqrt(ms + EPS) * w
        key = jax.random.key(seed)
        ks = jax.random.split(key, 10)
        s = 0.02
        return {'x': jax.random.normal(ks[0], (B, T, D), dtype=jnp.float32), 'W_DQ': jax.random.normal(ks[1], (DL, HD), dtype=jnp.float32) * s, 'W_UQ': jax.random.normal(ks[2], (HD, DL), dtype=jnp.float32) * s, 'W_DKV': jax.random.normal(ks[3], (2 * DL, HD), dtype=jnp.float32) * s, 'W_UKV': jax.random.normal(ks[4], (2 * HD, 2 * DL), dtype=jnp.float32) * s, 'W_QR': jax.random.normal(ks[5], (NR, HD), dtype=jnp.float32) * s, 'W_KR': jax.random.normal(ks[6], (NR, HD), dtype=jnp.float32) * s, 'W_O': jax.random.normal(ks[7], (HD, HD), dtype=jnp.float32) * s, 'q_norm_w': jnp.ones((HD,), dtype=jnp.float32), 'k_norm_w': jnp.ones((HD,), dtype=jnp.float32)}
    _L0_attn_b_in = _L0_attn_b_setup()

    def _L0_ffn_setup():
        import jax, jax.numpy as jnp
        import numpy as np
        D_MODEL = 128
        N_EXPERTS = 8
        TOP_K = 2
        HIDDEN = 4 * D_MODEL
        key = jax.random.key(seed)
        ks = jax.random.split(key, 6)
        B, S = (2, 256)
        x = jax.random.normal(ks[0], (B, S, D_MODEL), dtype=jnp.float32)
        shared_w1 = jax.random.normal(ks[1], (HIDDEN, D_MODEL), dtype=jnp.float32) * 0.02
        shared_w2 = jax.random.normal(ks[2], (D_MODEL, HIDDEN), dtype=jnp.float32) * 0.02
        experts_w1 = jax.random.normal(ks[3], (N_EXPERTS, HIDDEN, D_MODEL), dtype=jnp.float32) * 0.02
        experts_w2 = jax.random.normal(ks[4], (N_EXPERTS, D_MODEL, HIDDEN), dtype=jnp.float32) * 0.02
        gate_w = jax.random.normal(ks[5], (N_EXPERTS, D_MODEL), dtype=jnp.float32) * 0.02
        return {'x': x, 'shared_w1': shared_w1, 'shared_w2': shared_w2, 'experts_w1': experts_w1, 'experts_w2': experts_w2, 'gate_w': gate_w}
    _L0_ffn_in = _L0_ffn_setup()
    _d = {'L0_attn_a_hidden_states': _L0_attn_a_in['hidden_states'], 'L0_attn_a_in_proj_w': _L0_attn_a_in['in_proj_w'], 'L0_attn_a_conv_w': _L0_attn_a_in['conv_w'], 'L0_attn_a_conv_b': _L0_attn_a_in['conv_b'], 'L0_attn_a_A_log': _L0_attn_a_in['A_log'], 'L0_attn_a_dt_w': _L0_attn_a_in['dt_w'], 'L0_attn_a_dt_b': _L0_attn_a_in['dt_b'], 'L0_attn_a_B_w': _L0_attn_a_in['B_w'], 'L0_attn_a_C_w': _L0_attn_a_in['C_w'], 'L0_attn_a_D': _L0_attn_a_in['D'], 'L0_attn_a_ln_w': _L0_attn_a_in['ln_w'], 'L0_attn_a_ln_b': _L0_attn_a_in['ln_b'], 'L0_attn_a_out_proj_w': _L0_attn_a_in['out_proj_w'], 'L0_attn_b_W_DQ': _L0_attn_b_in['W_DQ'], 'L0_attn_b_W_UQ': _L0_attn_b_in['W_UQ'], 'L0_attn_b_W_DKV': _L0_attn_b_in['W_DKV'], 'L0_attn_b_W_UKV': _L0_attn_b_in['W_UKV'], 'L0_attn_b_W_QR': _L0_attn_b_in['W_QR'], 'L0_attn_b_W_KR': _L0_attn_b_in['W_KR'], 'L0_attn_b_W_O': _L0_attn_b_in['W_O'], 'L0_attn_b_q_norm_w': _L0_attn_b_in['q_norm_w'], 'L0_attn_b_k_norm_w': _L0_attn_b_in['k_norm_w'], 'L0_ffn_shared_w1': _L0_ffn_in['shared_w1'], 'L0_ffn_shared_w2': _L0_ffn_in['shared_w2'], 'L0_ffn_experts_w1': _L0_ffn_in['experts_w1'], 'L0_ffn_experts_w2': _L0_ffn_in['experts_w2'], 'L0_ffn_gate_w': _L0_ffn_in['gate_w']}
    _x0 = _d['L0_attn_a_hidden_states']
    _d['L0_attn_a_hidden_states'] = jax.random.normal(jax.random.fold_in(jax.random.key(seed), 1), (8, 256, 128), dtype=_x0.dtype)
    del _x0
    return _d

def reference(L0_attn_a_hidden_states, L0_attn_a_in_proj_w, L0_attn_a_conv_w, L0_attn_a_conv_b, L0_attn_a_A_log, L0_attn_a_dt_w, L0_attn_a_dt_b, L0_attn_a_B_w, L0_attn_a_C_w, L0_attn_a_D, L0_attn_a_ln_w, L0_attn_a_ln_b, L0_attn_a_out_proj_w, L0_attn_b_W_DQ, L0_attn_b_W_UQ, L0_attn_b_W_DKV, L0_attn_b_W_UKV, L0_attn_b_W_QR, L0_attn_b_W_KR, L0_attn_b_W_O, L0_attn_b_q_norm_w, L0_attn_b_k_norm_w, L0_ffn_shared_w1, L0_ffn_shared_w2, L0_ffn_experts_w1, L0_ffn_experts_w2, L0_ffn_gate_w):

    def _L0_attn_a_ref(hidden_states, in_proj_w, conv_w, conv_b, A_log, dt_w, dt_b, B_w, C_w, D, ln_w, ln_b, out_proj_w):
        import jax, jax.numpy as jnp
        import numpy as np
        D_MODEL = 128
        EXPAND = 2
        D_INNER = EXPAND * D_MODEL
        HEADDIM = 64
        NHEADS = D_INNER // HEADDIM
        D_STATE = 64
        D_CONV = 4
        BATCH = 2
        SEQ_LEN = 128
        LN_EPS = 1e-05

        def _layernorm(x, w, b):
            mu = jnp.mean(x, axis=-1, keepdims=True)
            var = jnp.var(x, axis=-1, keepdims=True)
            return (x - mu) * jax.lax.rsqrt(var + LN_EPS) * w + b

        def _forward(hidden_states, in_proj_w, conv_w, conv_b, A_log, dt_w, dt_b, B_w, C_w, D, ln_w, ln_b, out_proj_w):
            B_, L, _ = hidden_states.shape
            xz = hidden_states @ in_proj_w.T
            x, z = jnp.split(xz, 2, axis=-1)
            x_ncl = jnp.transpose(x, (0, 2, 1))
            x_conv = jax.lax.conv_general_dilated(x_ncl, conv_w, window_strides=(1,), padding=[(D_CONV - 1, 0)], dimension_numbers=('NCH', 'OIH', 'NCH'), feature_group_count=D_INNER)
            x_conv = x_conv + conv_b[None, :, None]
            x = jnp.transpose(x_conv, (0, 2, 1))
            x = jax.nn.silu(x)
            dt = jax.nn.softplus(x @ dt_w.T + dt_b)
            Bm = (x @ B_w.T).reshape(B_, L, NHEADS, D_STATE)
            Cm = (x @ C_w.T).reshape(B_, L, NHEADS, D_STATE)
            xh = x.reshape(B_, L, NHEADS, HEADDIM)
            A = -jnp.exp(A_log)
            h0 = jnp.zeros((B_, NHEADS, HEADDIM, D_STATE), x.dtype)

            def step(h, inp):
                x_t, dt_t, B_t, C_t = inp
                A_bar = jnp.exp(A[None, :] * dt_t)[..., None, None]
                h = A_bar * h + dt_t[..., None, None] * B_t[:, :, None, :] * x_t[..., None]
                y_t = jnp.einsum('bhpn,bhn->bhp', h, C_t) + D[None, :, None] * x_t
                return (h, y_t)
            xs = (jnp.transpose(xh, (1, 0, 2, 3)), jnp.transpose(dt, (1, 0, 2)), jnp.transpose(Bm, (1, 0, 2, 3)), jnp.transpose(Cm, (1, 0, 2, 3)))
            h_final, y = jax.lax.scan(step, h0, xs)
            y = jnp.transpose(y, (1, 0, 2, 3)).reshape(B_, L, D_INNER)
            y = _layernorm(y, ln_w, ln_b)
            y = y * jax.nn.silu(z)
            output = y @ out_proj_w.T
            return (output, h_final)

        def _reference_tuple_inner(hidden_states, in_proj_w, conv_w, conv_b, A_log, dt_w, dt_b, B_w, C_w, D, ln_w, ln_b, out_proj_w):
            return _forward(hidden_states, in_proj_w, conv_w, conv_b, A_log, dt_w, dt_b, B_w, C_w, D, ln_w, ln_b, out_proj_w)
        return _reference_tuple_inner(hidden_states, in_proj_w, conv_w, conv_b, A_log, dt_w, dt_b, B_w, C_w, D, ln_w, ln_b, out_proj_w)[0]

    def _L0_attn_b_ref(x, W_DQ, W_UQ, W_DKV, W_UKV, W_QR, W_KR, W_O, q_norm_w, k_norm_w):
        import jax, jax.numpy as jnp
        import numpy as np
        B, T, D = (2, 256, 128)
        H = 16
        HD = D // H
        DL = 64
        NR = 64
        EPS = 1.1920929e-07

        def _rms_norm(x, w):
            ms = jnp.mean(jnp.square(x), axis=-1, keepdims=True)
            return x * jax.lax.rsqrt(ms + EPS) * w
        b, t, d = x.shape
        scale = HD ** (-0.5)
        xh = x.reshape(b, t, H, HD).transpose(0, 2, 1, 3)
        c_q = jnp.einsum('bhtd,ld->bhtl', xh, W_DQ)
        q_c = jnp.einsum('bhtl,dl->bhtd', c_q, W_UQ)
        q_c_norm = _rms_norm(q_c, q_norm_w)
        q_r = jnp.einsum('bhtd,rd->bhtr', q_c_norm, W_QR)
        q = jnp.concatenate([q_c_norm, q_r], axis=-1)
        c_kv = jnp.einsum('bhtd,ld->bhtl', xh, W_DKV)
        kv = jnp.einsum('bhtl,dl->bhtd', c_kv, W_UKV)
        k_c, v_c = (kv[..., :HD], kv[..., HD:])
        k_c_norm = _rms_norm(k_c, k_norm_w)
        k_r = jnp.einsum('bhtd,rd->bhtr', xh, W_KR)
        k = jnp.concatenate([k_c_norm, k_r], axis=-1)
        scores = jnp.einsum('bhqd,bhkd->bhqk', q, k) * scale
        causal = jnp.triu(jnp.full((t, t), -jnp.inf, dtype=scores.dtype), k=1)
        attn = jax.nn.softmax(scores + causal, axis=-1)
        ctx = jnp.einsum('bhqk,bhkd->bhqd', attn, v_c)
        out = jnp.einsum('bhtd,od->bhto', ctx, W_O)
        return out.transpose(0, 2, 1, 3).reshape(b, t, d)

    def _L0_ffn_ref(x, shared_w1, shared_w2, experts_w1, experts_w2, gate_w):
        import jax, jax.numpy as jnp
        import numpy as np
        D_MODEL = 128
        N_EXPERTS = 8
        TOP_K = 2
        HIDDEN = 4 * D_MODEL
        B, S, D = x.shape
        T = B * S
        x_flat = x.reshape(T, D)
        shared = jnp.einsum('td,dh->th', x_flat, shared_w1.T)
        shared = jnp.einsum('th,hd->td', jax.nn.silu(shared), shared_w2.T)
        gate_logits = x_flat @ gate_w.T
        top_k_gates, top_k_idx = jax.lax.top_k(gate_logits, TOP_K)
        top_k_gates = jax.nn.softmax(top_k_gates, axis=1)
        gates = jnp.zeros((T, N_EXPERTS), dtype=x.dtype)
        gates = gates.at[jnp.arange(T)[:, None], top_k_idx].set(top_k_gates)
        h = jnp.einsum('td,ehd->teh', x_flat, experts_w1)
        expert_out = jnp.einsum('teh,edh->ted', jax.nn.silu(h), experts_w2)
        selected = jnp.einsum('ted,te->td', expert_out, gates)
        return (shared + selected).reshape(B, S, D)
    x = L0_attn_a_hidden_states
    x = x + _L0_attn_a_ref(_layernorm(x, axis=-1), L0_attn_a_in_proj_w, L0_attn_a_conv_w, L0_attn_a_conv_b, L0_attn_a_A_log, L0_attn_a_dt_w, L0_attn_a_dt_b, L0_attn_a_B_w, L0_attn_a_C_w, L0_attn_a_D, L0_attn_a_ln_w, L0_attn_a_ln_b, L0_attn_a_out_proj_w)
    x = x + _L0_ffn_ref(_layernorm(x, axis=-1), L0_ffn_shared_w1, L0_ffn_shared_w2, L0_ffn_experts_w1, L0_ffn_experts_w2, L0_ffn_gate_w)
    x = x + _L0_attn_b_ref(_layernorm(x, axis=-1), L0_attn_b_W_DQ, L0_attn_b_W_UQ, L0_attn_b_W_DKV, L0_attn_b_W_UKV, L0_attn_b_W_QR, L0_attn_b_W_KR, L0_attn_b_W_O, L0_attn_b_q_norm_w, L0_attn_b_k_norm_w)
    x = x + _L0_ffn_ref(_layernorm(x, axis=-1), L0_ffn_shared_w1, L0_ffn_shared_w2, L0_ffn_experts_w1, L0_ffn_experts_w2, L0_ffn_gate_w)
    return x

_drawn_inputs = setup_inputs


def setup_inputs(seed=0):
    import zlib

    import numpy as np

    out = dict(_drawn_inputs(seed))
    spreads = {'L0_attn_a_A_log': (0.0, 2.0),
     'L0_attn_a_D': (1.0, 0.6),
     'L0_attn_a_ln_w': (1.0, 0.6),
     'L0_attn_a_ln_b': (0.0, 0.8),
     'L0_attn_b_q_norm_w': (1.0, 0.6),
     'L0_attn_b_k_norm_w': (1.0, 0.6)}
    factors = {'L0_attn_a_conv_b': 6.307,
     'L0_attn_a_dt_w': 64.0,
     'L0_attn_a_dt_b': 64.0,
     'L0_attn_a_B_w': 52.168,
     'L0_attn_a_C_w': 64.0,
     'L0_attn_b_W_DQ': 8.0,
     'L0_attn_b_W_UQ': 8.0,
     'L0_attn_b_W_DKV': 8.0,
     'L0_attn_b_W_UKV': 8.0,
     'L0_attn_b_W_QR': 8.0,
     'L0_attn_b_W_KR': 8.0,
     'L0_attn_b_W_O': 8.0}
    for name, (base, spread) in spreads.items():
        noise = np.random.default_rng([zlib.crc32(name.encode()), seed]).standard_normal(out[name].shape)
        drawn = base * np.exp(spread * noise) if base else spread * noise
        out[name] = jnp.asarray(drawn.astype(out[name].dtype))
    for name, factor in factors.items():
        out[name] = (out[name] * factor).astype(out[name].dtype)
    return out
```

```python
from contextlib import ExitStack

import concourse.bass as bass
from concourse import mybir

F32 = mybir.dt.float32
F32R = mybir.dt.float32r
BF16 = mybir.dt.bfloat16
U32 = mybir.dt.uint32
ALU = mybir.AluOpType
ACT = mybir.ActivationFunctionType
AX = mybir.AxisListType
ds = bass.ds

P = 128
LN_EPS = 1e-5
RMS_EPS = 1.1920929e-07
MASKED = -1e30


def hybrid_kernel(nc, x, w_in, conv_w, conv_b, a_log, dt_w, dt_b, b_w, c_w, d_skip, ln_w, ln_b, w_out,
                  w_dq, w_uq_t, w_dkv, w_ukv_t, w_qr, w_kr, w_o_t, qn_w, kn_w,
                  moe_w1, moe_w2, gate_w, out):
    B, T, D = 8, 256, x.shape[1]
    NT = x.shape[0] // P
    TB = T // P
    DI = w_out.shape[0] * w_out.shape[1]
    KI = DI // P
    NH = a_log.shape[1]
    HP = DI // NH
    TAPS = conv_w.shape[2]
    H = 16
    HD = D // H
    NG = H // 4
    NE = gate_w.shape[1]
    HID = moe_w1.shape[2]
    CH = HID // P
    TG = 4
    GT = NT // TG
    GN = GT * P
    XRW = P + NH
    assert B * TB == NT and KI == 2 and NH == 4 and TB == 2 and NE == 8 and CH == 4

    with ExitStack() as ctx:
        def sb(name, shape, dt=F32, stack=ctx):
            return stack.enter_context(nc.sbuf_tensor(name, shape, dt))

        def sem(name):
            return ctx.enter_context(nc.semaphore(name))

        PS = ctx.enter_context(nc.psum_tensor("PS", [P, 8, 512], F32))

        X = sb("X", [P, NT, D])
        ident = sb("ident", [P, 2 * P])
        stats = sb("stats", [P, NT, 6])
        mean = sb("mean", [P, NT])
        var = sb("var", [P, NT])
        mtmp = sb("mtmp", [P, 4, NT])
        rstd = sb("rstd", [P, NT])
        std = sb("std", [P, NT])

        raw = sb("raw", [P, 2, HID])
        gate_w_s = sb("gate_w_s", [P, NE])
        iota = sb("iota", [P, NE])
        iota_i = sb("iota_i", [P, NE], mybir.dt.int32)
        NSEC = 4
        SLOT = 32
        w_dq_s = sb("w_dq_s", [64, HD]); w_uq_s = sb("w_uq_s", [64, HD])
        w_dkv_s = sb("w_dkv_s", [P, HD]); w_ukv_s = sb("w_ukv_s", [P, 2 * HD])
        w_qr_s = sb("w_qr_s", [64, HD]); w_kr_s = sb("w_kr_s", [64, HD]); w_o_s = sb("w_o_s", [HD, HD])
        row_qk = sb("row_qk", [P, 3, HD])
        small = sb("small", [HD, NSEC * HD])
        av = sb("av", [HD, HD])
        rep8 = sb("rep8", [HD, H, HD])
        wa_rep = sb("wa_rep", [P, NSEC * HD])
        head_of = sb("head_of", [P, H])
        w_all = sb("w_all", [P, NSEC, H, HD])
        ident_b = sb("ident_b", [P, P], BF16)
        mask_ts = sb("mask_ts", [P, P], BF16)
        mask_st = sb("mask_st", [P, P], BF16)

        mamba = ExitStack()
        w_in_s = sb("w_in_s", [P, 2 * DI], stack=mamba)
        conv_w_s = sb("conv_w_s", [P, KI, TAPS], stack=mamba)
        conv_b_s = sb("conv_b_s", [P, KI], stack=mamba)
        idt_w = sb("idt_w", [P, KI, XRW], stack=mamba)
        b_w_s = sb("b_w_s", [P, KI, DI], stack=mamba)
        c_w_s = sb("c_w_s", [P, KI, DI], stack=mamba)
        w_out_s = sb("w_out_s", [P, KI, D], stack=mamba)
        row_nh = sb("row_nh", [P, 3, NH], stack=mamba)
        row_ln = sb("row_ln", [P, 2, DI], stack=mamba)
        neg_a = sb("neg_a", [P, NH], stack=mamba)
        xn = sb("xn", [P, 2, TB, D], stack=mamba)
        xn_t = sb("xn_t", [P, 2, T], stack=mamba)
        x_pad = sb("x_pad", [P, 2, KI, TAPS - 1 + T], stack=mamba)
        conv_o = sb("conv_o", [P, 2, KI, T], stack=mamba)
        xs_t = sb("xs_t", [P, 2, KI, T], stack=mamba)
        z_act = sb("z_act", [P, 2, TB, DI], stack=mamba)
        XST = sb("XST", [P, KI, B * T], stack=mamba)
        XR = sb("XR", [P, NT, KI, XRW], stack=mamba)
        ZW = sb("ZW", [P, NT, DI], stack=mamba)
        ZB = sb("ZB", [P, NT, DI], stack=mamba)
        DT = sb("DT", [P, NT, NH], stack=mamba)
        AB = sb("AB", [P, NT, NH], stack=mamba)
        tmp = [sb(f"dt_tmp{i}", [P, NT, NH], stack=mamba) for i in range(6)]
        b_t = sb("b_t", [P, KI, T], stack=mamba)
        c_z = sb("c_z", [P, NH, T], stack=mamba)
        ab_b = sb("ab_b", [P, TB, NH], stack=mamba)
        xdt = sb("xdt", [P, TB, DI], stack=mamba)
        dx = sb("dx", [P, TB, DI], stack=mamba)
        dec0 = sb("dec0", [P, KI, 2, T], stack=mamba)
        dec1 = sb("dec1", [P, KI, 2, P], stack=mamba)
        w0 = sb("w0", [P, KI, 2, T], stack=mamba)
        w1 = sb("w1", [P, KI, 2, P], stack=mamba)
        y = sb("y", [P, TB, DI], stack=mamba)
        yst = sb("yst", [P, TB, 6], stack=mamba)
        ymv = sb("ymv", [P, TB, 2], stack=mamba)
        ysd = sb("ysd", [P, TB], stack=mamba)
        yrs = sb("yrs", [P, TB], stack=mamba)
        yn = sb("yn", [P, TB, DI], stack=mamba)
        yw = sb("yw", [P, TB, DI], stack=mamba)
        g = sb("g", [P, TB, DI], stack=mamba)
        g_t = sb("g_t", [P, KI, T], stack=mamba)
        mamba.close()

        moe = ExitStack()
        XH = sb("XH", [P, NT * P], F32R, stack=moe)
        XL = sb("XL", [P, NT * P], F32R, stack=moe)
        acc = sb("acc", [P, NT * P], stack=moe)
        w_hi = sb("w_hi", [P, 2, 2, HID], F32R, stack=moe)
        w_lo = sb("w_lo", [P, 2, 2, HID], F32R, stack=moe)
        h_f = sb("h_f", [P, 2, 2, 2 * GN], stack=moe)
        h_hi = sb("h_hi", [P, 2, 2, 2 * GN], F32R, stack=moe)
        h_lo = sb("h_lo", [P, 2, 2, 2 * GN], F32R, stack=moe)
        gates_b = sb("gates_b", [P, 2, NT * P], stack=moe)
        gy = sb("gy", [P, 2, GN], stack=moe)
        xn4 = sb("xn4", [P, 2, GT, D], stack=moe)
        xt4 = sb("xt4", [P, 2, GN], stack=moe)
        logits = sb("logits", [P, NT, NE], stack=moe)
        top = sb("top", [P, NT, 8], stack=moe)
        top_i = sb("top_i", [P, NT, 8], U32, stack=moe)
        top_if = sb("top_if", [P, NT, 2], stack=moe)
        top_g = sb("top_g", [P, 4, NT], stack=moe)
        pick = sb("pick", [P, 2, NT, NE], stack=moe)
        gates = sb("gates", [P, NE, NT], stack=moe)
        gates_t = sb("gates_t", [P, P], stack=moe)
        moe.close()
        gates_d = nc.dram_tensor("gates_d", (P, P), F32).ap()

        attn = ExitStack()
        QKVM = sb("QKVM", [P, NT, NSEC * D], stack=attn)
        xa = sb("xa", [P, 2, TB, D], stack=attn)
        xa_t = sb("xa_t", [P, 2, T], stack=attn)
        sq = sb("sq", [P, 2, TB, 2 * D], stack=attn)
        ss = sb("ss", [P, NT, 2 * H], stack=attn)
        rr = sb("rr", [P, NT, 2 * H], stack=attn)
        q1 = sb("q1", [P, TB, D], stack=attn)
        kn = sb("kn", [P, 3, TB, D], stack=attn)
        q_pad = sb("q_pad", [P, 2, TB, H, SLOT], stack=attn)
        k_pad = sb("k_pad", [P, 2, TB, H, SLOT], stack=attn)
        v_pad = sb("v_pad", [P, 2, TB, H, SLOT], stack=attn)
        q_t = sb("q_t", [P, 2, NG, T], F32R, stack=attn)
        k_z = sb("k_z", [P, 2, NG, 4, T], F32R, stack=attn)
        neg_max = sb("neg_max", [P, TB, H], stack=attn)
        probs = sb("probs", [P, 2, 4, T + P], stack=attn)
        o_t = sb("o_t", [P, NG, T], stack=attn)
        den = sb("den", [P, TB, H], stack=attn)
        o_r = sb("o_r", [P, TB, D], stack=attn)
        attn.close()

        s_x = sem("s_x"); s_w = sem("s_w"); s_w_in = sem("s_w_in"); s_tap0 = sem("s_tap0"); s_const = sem("s_const"); s_out = sem("s_out")
        s_phase = sem("s_phase")
        s_ln = sem("s_ln"); s_lnv = sem("s_lnv"); s_std = sem("s_std")
        s_xn = sem("s_xn"); s_xn_ps = sem("s_xn_ps"); s_xn_t = sem("s_xn_t")
        s_xc_ps = sem("s_xc_ps"); s_z_ps = sem("s_z_ps"); s_xpad = sem("s_xpad"); s_z = sem("s_z")
        s_zw = sem("s_zw"); s_tap = sem("s_tap"); s_xs_t = sem("s_xs_t"); s_xst = sem("s_xst")
        s_xr_ps = sem("s_xr_ps"); s_xr = sem("s_xr")
        s_dtv = sem("s_dtv"); s_dta = sem("s_dta")
        s_bc_ps = sem("s_bc_ps"); s_bc = sem("s_bc"); s_ab = sem("s_ab"); s_xdt = sem("s_xdt")
        s_g_ps = sem("s_g_ps"); s_dec = sem("s_dec"); s_wq = sem("s_wq")
        s_y_ps = sem("s_y_ps"); s_y = sem("s_y"); s_ymv = sem("s_ymv")
        s_ysd = sem("s_ysd"); s_yrs = sem("s_yrs"); s_yn = sem("s_yn"); s_yw = sem("s_yw"); s_g = sem("s_g")
        s_gt_ps = sem("s_gt_ps"); s_gt = sem("s_gt"); s_o_ps = sem("s_o_ps"); s_o = sem("s_o")

        s_raw = sem("s_raw"); s_split = sem("s_split"); s_xn4 = sem("s_xn4"); s_xt_ps = sem("s_xt_ps")
        s_xt = sem("s_xt"); s_xl = sem("s_xl"); s_lg_ps = sem("s_lg_ps"); s_lg = sem("s_lg")
        s_top = sem("s_top"); s_e = sem("s_e"); s_gates = sem("s_gates"); s_gates_ps = sem("s_gates_ps")
        s_gates_t = sem("s_gates_t"); s_gates_d = sem("s_gates_d"); s_gb = [sem(f"s_gb{i}") for i in range(2)]
        s_up = sem("s_up"); s_silu = sem("s_silu"); s_hi = sem("s_hi"); s_lo = sem("s_lo")
        s_down = sem("s_down"); s_gated = sem("s_gated"); s_acc = sem("s_acc")
        s_acc_ps = sem("s_acc_ps"); s_res = sem("s_res")
        s_aw = sem("s_aw"); s_ac = sem("s_ac"); s_aw_ps = sem("s_aw_ps"); s_aw_c = sem("s_aw_c"); s_wa = sem("s_wa")
        s_xa = sem("s_xa"); s_xa_ps = sem("s_xa_ps"); s_xa_t = sem("s_xa_t"); s_qkvm_ps = sem("s_qkvm_ps")
        s_qkvm = sem("s_qkvm"); s_sq = sem("s_sq"); s_ss = sem("s_ss"); s_rs = sem("s_rs"); s_rr = sem("s_rr")
        s_kn = sem("s_kn"); s_q1 = sem("s_q1"); s_kpad = sem("s_kpad"); s_qpad = sem("s_qpad"); s_qf_ps = sem("s_qf_ps"); s_qf = [sem(f"s_qf{i}") for i in range(2)]; s_res_a = sem("s_res_a"); s_v = sem("s_v"); s_z0 = sem("s_z0")
        s_kt_ps = sem("s_kt_ps"); s_qt_ps = sem("s_qt_ps"); s_kz = sem("s_kz"); s_qt = sem("s_qt")
        s_p1 = sem("s_p1"); s_max = sem("s_max"); s_nm = sem("s_nm"); s_p2 = sem("s_p2"); s_exp = sem("s_exp")
        s_pv = sem("s_pv"); s_ot = sem("s_ot"); s_or_ps = sem("s_or_ps"); s_or = sem("s_or"); s_den = sem("s_den")

        block = ctx.enter_context(nc.Block())
        UNITS = TG * (1 + NE)
        LAST_PHASE = 5
        LAST_LN = 4

        def wait(eng, s, n):
            if not (isinstance(n, int) and n <= 0):
                eng.wait_ge(s, n)

        def pipelined(eng, step):
            step(0, 0, True, False)
            step(1, 1, False, False)
            with eng.Fori(1, B // 2 - 1) as i:
                step(2 * i, 0, False, False)
                step(2 * i + 1, 1, False, False)
            step(B - 2, 0, False, False)
            step(B - 1, 1, False, True)

        def end_phase(eng, n):
            eng.drain().then_inc(s_phase, 1)
            eng.wait_ge(s_phase, 4 * n)

        @block.sync
        def _(sp):
            sp.dma_start(X[:, :, :], x.rearrange("(j p) d -> p j d", p=P)).then_inc(s_x, 16)
            sp.dma_start(w_in_s[:, :], w_in).then_inc(s_w_in, 16)
            for dst, src in ((conv_w_s[:, :, :], conv_w), (conv_b_s[:, :], conv_b),
                             (idt_w[:, :, P:XRW], dt_w), (b_w_s[:, :, :], b_w), (c_w_s[:, :, :], c_w),
                             (w_out_s[:, :, :], w_out.rearrange("k p d -> p k d"))):
                sp.dma_start(dst, src).then_inc(s_w, 16)
            for i, src in enumerate((a_log, dt_b, d_skip)):
                sp.dma_start(row_nh[:, i, :], src.broadcast_to((P, NH))).then_inc(s_w, 16)
            for i, src in enumerate((ln_w, ln_b)):
                sp.dma_start(row_ln[:, i, :], src.broadcast_to((P, DI))).then_inc(s_w, 16)
            for dst, src in ((gate_w_s, gate_w), (w_dq_s, w_dq), (w_uq_s, w_uq_t), (w_dkv_s, w_dkv),
                             (w_ukv_s, w_ukv_t), (w_qr_s, w_qr), (w_kr_s, w_kr), (w_o_s, w_o_t)):
                sp.dma_start(dst[:, :], src).then_inc(s_aw, 16)
            for i, src in enumerate((qn_w, kn_w)):
                sp.dma_start(row_qk[:, i, :], src.broadcast_to((P, HD))).then_inc(s_aw, 16)

            def weights(m, k):
                if not (m == 0 and isinstance(k, int) and k == 0):
                    sp.wait_ge(s_split, 2 * ((1 + NE) * m + k))
                sp.dma_start(raw[:, 0, :], moe_w1[ds(k, 1), :, :].rearrange("e p n -> p (e n)")).then_inc(s_raw, 16)
                sp.dma_start(raw[:, 1, :], moe_w2[ds(k, 1), :, :, :].rearrange("e p c n -> p (e c n)")).then_inc(s_raw, 16)

            def gates_of(m, k, o):
                if not (isinstance(k, int) and k <= 2):
                    sp.wait_ge(s_gated, UNITS * m + TG * (k - 1))
                sp.dma_start(gates_b[:, o, :], gates_d[ds(NT * (k - 1), NT), :]
                             .rearrange("(o j) p -> o (j p)", o=1).broadcast_to((P, NT * P))).then_inc(s_gb[o], 16)

            for m in range(2):
                weights(m, 0)
                weights(m, 1)
                sp.wait_ge(s_gates_t, m + 1)
                sp.dma_start(gates_d, gates_t[:, :]).then_inc(s_gates_d, 16)
                sp.wait_ge(s_gates_d, 16 * (m + 1))
                for k in range(1, 3):
                    gates_of(m, k, k - 1)
                    weights(m, k + 1)
                with sp.Fori(1, NE // 2 - 1) as i:
                    for o in range(2):
                        gates_of(m, 2 * i + 1 + o, o)
                        weights(m, 2 * i + 2 + o)
                gates_of(m, NE - 1, 0)
                weights(m, NE)
                gates_of(m, NE, 1)
            sp.wait_ge(s_phase, 4 * LAST_PHASE)
            sp.dma_start(out.rearrange("(j p) d -> p j d", p=P), X[:, :, :]).then_inc(s_out, 16)
            sp.wait_ge(s_out, 16)

        W_ALL = 16 * 11

        @block.gpsimd
        def _(pool):
            def moe_pool(m, phase):
                def split(k, o):
                    pool.wait_ge(s_raw, 32 * ((1 + NE) * m + k + 1))
                    if not (isinstance(k, int) and k < 2):
                        pool.wait_ge(s_down, UNITS * m + TG * (k - 1))
                    pool.tensor_tensor(w_hi[:, o, :, :], raw[:, :, :], ident[:, P:P + 1].unsqueeze(2).broadcast_to((P, 2, HID)),
                                       ALU.add).then_inc(s_split, 1)
                    pool.wait_ge(s_split, 2 * ((1 + NE) * m + k) + 1)
                    pool.tensor_tensor(w_lo[:, o, :, :], raw[:, :, :], w_hi[:, o, :, :].bitcast(F32),
                                       ALU.subtract).then_inc(s_split, 1)

                def add(n, tg, start=False):
                    pool.wait_ge(s_gated, n + 1)
                    part = acc[:, tg * GN:(tg + 1) * GN]
                    if start:
                        zero = ident[:, P:P + 1].broadcast_to((P, GN))
                        pool.tensor_tensor(part, gy[:, tg % 2, :], zero, ALU.add).then_inc(s_acc, 1)
                        return
                    pool.wait_ge(s_acc, n - TG + 1)
                    pool.tensor_tensor(part, part, gy[:, tg % 2, :], ALU.add).then_inc(s_acc, 1)

                split(0, 0)
                split(1, 1)
                for tg in range(TG):
                    add(UNITS * m + tg, tg, start=True)
                with pool.Fori(0, NE // 2 - 1) as i:
                    for o in range(2):
                        for tg in range(TG):
                            add(UNITS * m + TG * (2 * i + 1 + o) + tg, tg)
                            if tg == 0:
                                split(2 * i + 2 + o, o)
                for o in range(2):
                    for tg in range(TG):
                        add(UNITS * m + TG * (NE - 1 + o) + tg, tg)
                        if tg == 0 and o == 0:
                            split(NE, 0)
                end_phase(pool, phase)

            def attn_pool():
                pool.memset(k_z[:, :, :, :, :].bitcast(F32), 0.0).then_inc(s_z0, 1)
                for pad in (q_pad, k_pad, v_pad):
                    pool.memset(pad[:, :, :, :, :], 0.0).then_inc(s_z0, 1)
                pool.wait_ge(s_z0, 4)
                pool.memset(k_pad[:, :, :, :, 3 * HD:3 * HD + 2], 1.0).then_inc(s_z0, 1)
                pool.memset(v_pad[:, :, :, :, HD:HD + 1], 1.0).then_inc(s_z0, 1)

                def squares(b, o, first, last):
                    for c in range(TB):
                        pool.wait_ge(s_qkvm, TB * b + c + 1)
                        if not first:
                            wait(pool, s_ss, TB * (b - 1))
                        qk = QKVM[:, ds(TB * b + c, 1), 0:2 * D].rearrange("p o n -> p (o n)")
                        pool.tensor_tensor(sq[:, o, c, :], qk, qk, ALU.mult).then_inc(s_sq, 1)

                pipelined(pool, squares)
                pool.wait_ge(s_rr, 1)

                def prepare(b, o, first, last):
                    if isinstance(b, int) and b == 1:
                        pool.wait_ge(s_rr, 2)

                    def section(i):
                        return QKVM[:, ds(TB * b, TB), i * D:(i + 1) * D].rearrange("p c (h e) -> p c h e", h=H)

                    def inverse(i):
                        return rr[:, ds(TB * b, TB), i * H:(i + 1) * H].unsqueeze(3).broadcast_to((P, TB, H, HD))

                    def heads(t):
                        return t.rearrange("p c (h e) -> p c h e", h=H)

                    def slots(pad, a):
                        return pad[:, o, :, :, a * HD:(a + 1) * HD].rearrange("p c h e -> p (c h) e")

                    def flat(t):
                        return t.rearrange("p c (h e) -> p (c h) e", h=H)

                    zero = ident[:, P:P + 1].unsqueeze(2)
                    wait(pool, s_kpad, 2 * b)
                    pool.tensor_tensor(heads(kn[:, 0, :, :]), section(1), inverse(1), ALU.mult).then_inc(s_kn, 1)
                    pool.wait_ge(s_kn, 3 * b + 1)
                    pool.tensor_tensor(kn[:, 1, :, :].rearrange("p c (h e) -> p (c h) e", h=H),
                                       kn[:, 0, :, :].rearrange("p c (h e) -> p (c h) e", h=H),
                                       row_qk[:, 2:3, :].broadcast_to((P, TB * H, HD)), ALU.mult).then_inc(s_kn, 1)
                    pool.wait_ge(s_kn, 3 * b + 2)
                    pool.tensor_tensor(heads(kn[:, 2, :, :]), heads(kn[:, 1, :, :]), section(3), ALU.add).then_inc(s_kn, 1)
                    if not first:
                        wait(pool, s_kt_ps, b - 1)
                    pool.wait_ge(s_kn, 3 * b + 3)
                    twice = k_pad[:, o, :, :, 0:2 * HD].rearrange("p c h (a e) -> p (c h) a e", a=2)
                    pool.tensor_tensor(twice.bitcast(F32R), flat(kn[:, 2, :, :]).unsqueeze(2).broadcast_to((P, TB * H, 2, HD)),
                                       zero.unsqueeze(3).broadcast_to((P, TB * H, 2, HD)), ALU.add).then_inc(s_kpad, 1)
                    pool.wait_ge(s_kpad, 2 * b + 1)
                    pool.tensor_tensor(slots(k_pad, 2).bitcast(F32R), flat(kn[:, 2, :, :]), slots(k_pad, 0),
                                       ALU.subtract).then_inc(s_kpad, 1)
                    wait(pool, s_qpad, 2 * b)
                    pool.tensor_tensor(heads(q1[:, :, :]), section(0), inverse(0), ALU.mult).then_inc(s_q1, 1)
                    if not first:
                        wait(pool, s_qf_ps, 2 * (b - 1))
                    pool.wait_ge(s_q1, 2 * b + 1)
                    ends = q_pad[:, o, :, :, 0:3 * HD].rearrange("p c h (a e) -> p (c h) a e", a=3)[:, :, 0:3:2, :]
                    pool.tensor_tensor(ends.bitcast(F32R), flat(q1[:, :, :]).unsqueeze(2).broadcast_to((P, TB * H, 2, HD)),
                                       zero.unsqueeze(3).broadcast_to((P, TB * H, 2, HD)), ALU.add).then_inc(s_qpad, 1)
                    pool.memset(q_pad[:, o, :, :, 3 * HD:3 * HD + 2], 0.0).then_inc(s_q1, 1)
                    pool.wait_ge(s_qpad, 2 * b + 1)
                    pool.tensor_tensor(slots(q_pad, 1).bitcast(F32R), flat(q1[:, :, :]), slots(q_pad, 0),
                                       ALU.subtract).then_inc(s_qpad, 1)
                    if not first:
                        wait(pool, s_pv, NG * (b - 1))
                    pool.tensor_tensor(v_pad[:, o, :, :, 0:HD], section(2), zero.unsqueeze(3).broadcast_to((P, TB, H, HD)),
                                       ALU.add).then_inc(s_v, 1)

                pipelined(pool, prepare)

            pool.memset(ident[:, :], 0.0).then_inc(s_const, 1)
            pool.memset(x_pad[:, :, :, 0:TAPS - 1], 0.0).then_inc(s_const, 1)
            pool.memset(c_z[:, :, :], 0.0).then_inc(s_const, 1)
            pool.wait_ge(s_const, 3)
            pool.affine_select(out=ident[:, 0:P], in_=ident[:, 0:P], compare_op=ALU.not_equal, fill=1.0,
                               base=0, pattern=[[-1, P]], channel_multiplier=1).then_inc(s_const, 1)
            pool.wait_ge(s_const, 4)
            pool.iota(iota_i[:, :], pattern=[[1, NE]], base=0, channel_multiplier=0).then_inc(s_ac, 1)
            pool.memset(mask_ts[:, :], 0.0).then_inc(s_ac, 1)
            pool.memset(mask_st[:, :], 0.0).then_inc(s_ac, 1)
            pool.memset(head_of[:, :], 1.0).then_inc(s_ac, 1)
            pool.wait_ge(s_ac, 4)
            pool.tensor_copy(iota[:, :], iota_i[:, :]).then_inc(s_ac, 1)
            pool.affine_select(out=mask_ts[:, :], in_=mask_ts[:, :], compare_op=ALU.is_ge, fill=MASKED,
                               base=0, pattern=[[-1, P]], channel_multiplier=1).then_inc(s_ac, 1)
            pool.affine_select(out=mask_st[:, :], in_=mask_st[:, :], compare_op=ALU.is_ge, fill=MASKED,
                               base=0, pattern=[[1, P]], channel_multiplier=-1).then_inc(s_ac, 1)
            pool.affine_select(out=head_of[:, :], in_=head_of[:, :], compare_op=ALU.is_ge, fill=0.0,
                               base=0, pattern=[[-HD, H]], channel_multiplier=1).then_inc(s_ac, 1)
            pool.wait_ge(s_ac, 8)
            pool.affine_select(out=head_of[:, :], in_=head_of[:, :], compare_op=ALU.is_ge, fill=0.0,
                               base=HD - 1, pattern=[[HD, H]], channel_multiplier=-1).then_inc(s_ac, 1)
            pool.tensor_copy(ident_b[:, :], ident[:, 0:P]).then_inc(s_ac, 1)
            pool.tensor_copy(rep8[:, :, :], ident[0:HD, 0:HD].unsqueeze(1).broadcast_to((HD, H, HD))).then_inc(s_ac, 1)
            pool.wait_ge(s_w, W_ALL)
            for k in range(KI):
                pool.tensor_copy(idt_w[:, k, 0:P], ident[:, 0:P]).then_inc(s_const, 1)
            def z_parts(b, o, first, last):
                pool.wait_ge(s_z, b + 1)
                for i, dst in enumerate((ZW, ZB)):
                    pool.tensor_tensor(dst[:, ds(TB * b, TB), :], z_act[:, o, :, :],
                                       row_ln[:, i:i + 1, :].broadcast_to((P, TB, DI)), ALU.mult).then_inc(s_zw, 1)

            pipelined(pool, z_parts)
            end_phase(pool, 1)

            def inputs_of(b):
                if not (isinstance(b, int) and b == 0):
                    pool.wait_ge(s_y, TB * b)
                for c in range(TB):
                    rows = XR[:, ds(TB * b + c, 1), :, 0:P].rearrange("p o k (h e) -> p (o k) h e", h=NH // KI)
                    pool.tensor_tensor(
                        xdt[:, c, :].rearrange("p (k h e) -> p k h e", k=KI, h=NH // KI), rows,
                        DT[:, ds(TB * b + c, 1), :].rearrange("p o (k h) -> p (o k) h", k=KI).unsqueeze(3)
                        .broadcast_to((P, KI, NH // KI, HP)), ALU.mult).then_inc(s_xdt, 1)
                    pool.tensor_tensor(
                        dx[:, c, :].rearrange("p (k h e) -> p k h e", k=KI, h=NH // KI), rows,
                        row_nh[:, 2, :].rearrange("p (k h) -> p k h", k=KI).unsqueeze(3)
                        .broadcast_to((P, KI, NH // KI, HP)), ALU.mult).then_inc(s_xdt, 1)
                    if c == 0:
                        pool.tensor_copy(ab_b[:, :, :], AB[:, ds(TB * b, TB), :]).then_inc(s_ab, 1)

            def gated(b):
                pool.wait_ge(s_yn, b + 1)
                pool.tensor_tensor(yw[:, :, :], yn[:, :, :], ZW[:, ds(TB * b, TB), :], ALU.mult).then_inc(s_yw, 1)
                pool.wait_ge(s_yw, b + 1)
                wait(pool, s_gt_ps, b)
                pool.tensor_tensor(g[:, :, :], yw[:, :, :], ZB[:, ds(TB * b, TB), :], ALU.add).then_inc(s_g, 1)

            inputs_of(0)
            inputs_of(1)
            gated(0)
            with pool.Fori(1, B - 1) as b:
                inputs_of(b + 1)
                gated(b)
            gated(B - 1)
            end_phase(pool, 2)
            moe_pool(0, 3)
            attn_pool()
            end_phase(pool, 4)
            moe_pool(1, 5)

        @block.scalar
        def _(act):
            act.wait_ge(s_lnv, 1)
            act.activation(std[:, :], var[:, :], ACT.Sqrt).then_inc(s_std, 1)

            def front(b, o):
                act.wait_ge(s_xn_ps, b + 1)
                act.copy(xn_t[:, o, :], PS[:, 5 * o, 0:T]).then_inc(s_xn_t, 1)

            def split_up(b, o):
                act.wait_ge(s_xc_ps, b + 1)
                wait(act, s_tap, KI * (TAPS - 1) * (b - 1))
                xc = PS[:, 1 + 5 * o, :].rearrange("p (k t) -> p k t", k=KI)
                act.copy(x_pad[:, o, :, TAPS - 1:], xc).then_inc(s_xpad, 1)
                for k in range(KI):
                    act.mul(conv_o[:, o, k, :], xc[:, k, :], conv_w_s[:, k, TAPS - 1:TAPS]).then_inc(s_tap0, 1)
                act.wait_ge(s_z_ps, b + 1)
                wait(act, s_zw, 2 * (b - 1))
                act.activation(z_act[:, o, :, :], PS[:, 2 + 5 * o, :].rearrange("p (c n) -> p c n", c=TB), ACT.Silu).then_inc(s_z, 1)

            def rows_copy(b):
                act.wait_ge(s_xr_ps, b + 1)
                for c in range(TB):
                    act.copy(XR[:, ds(TB * b + c, 1), :, :].rearrange("p o k n -> p (o k) n"),
                             PS[:, 3 + c, 0:KI * XRW].rearrange("p (k n) -> p k n", k=KI)).then_inc(s_xr, 1)

            def front_step(b, o, first, last):
                if not last:
                    front(b + 1, 1 - o)
                if not first:
                    rows_copy(b - 1)
                if not last:
                    split_up(b + 1, 1 - o)
                act.wait_ge(s_tap, KI * (TAPS - 1) * (b + 1))
                wait(act, s_xst, b - 1)
                for k in range(KI):
                    act.activation(xs_t[:, o, k, :], conv_o[:, o, k, :], ACT.Silu, bias=conv_b_s[:, k:k + 1]).then_inc(s_xs_t, 1)

            act.wait_ge(s_w, W_ALL)
            front(0, 0)
            split_up(0, 0)
            pipelined(act, front_step)
            rows_copy(B - 1)
            act.wait_ge(s_dtv, 3)
            act.activation(tmp[2][:, :, :], tmp[1][:, :, :], ACT.Exp).then_inc(s_dta, 1)
            act.activation(neg_a[:, :], row_nh[:, 0, :], ACT.Exp).then_inc(s_dta, 1)
            act.wait_ge(s_dtv, 4)
            act.activation(tmp[4][:, :, :], tmp[3][:, :, :], ACT.Ln).then_inc(s_dta, 1)
            act.wait_ge(s_dtv, 12)
            act.activation(AB[:, :, :], tmp[1][:, :, :], ACT.Exp, scale=-1.0).then_inc(s_dta, 1)
            end_phase(act, 1)

            def bc_copy(b):
                act.wait_ge(s_bc_ps, b + 1)
                act.copy(b_t[:, :, :], PS[:, 0, :].rearrange("p (q t) -> p q t", q=KI)).then_inc(s_bc, 1)
                for r in range(2):
                    half = slice(HP * r, HP * (r + 1))
                    act.copy(c_z[half, r:NH:2, :], PS[half, 1, :].rearrange("p (q t) -> p q t", q=KI)).then_inc(s_bc, 1)

            def gate_copy(b):
                act.wait_ge(s_gt_ps, b + 1)
                act.copy(g_t[:, :, :], PS[:, 0, :].rearrange("p (k t) -> p k t", k=KI)).then_inc(s_gt, 1)

            def y_std(b):
                act.wait_ge(s_ymv, TB * (b + 1))
                act.activation(ysd[:, :], ymv[:, :, 1], ACT.Sqrt, bias=LN_EPS).then_inc(s_ysd, 1)

            bc_copy(0)
            bc_copy(1)
            y_std(0)
            with act.Fori(1, B - 1) as b:
                gate_copy(b - 1)
                bc_copy(b + 1)
                y_std(b)
            gate_copy(B - 2)
            y_std(B - 1)
            gate_copy(B - 1)
            end_phase(act, 2)

            def moe_act(m, ln, phase):
                act.wait_ge(s_lnv, ln)
                act.activation(std[:, :], var[:, :], ACT.Sqrt).then_inc(s_std, 1)
                for tg in range(TG):
                    n = TG * m + tg
                    act.wait_ge(s_xt_ps, n + 1)
                    wait(act, s_lg_ps, n - 1)
                    wait(act, s_xl, 2 * (n - 1))
                    act.copy(xt4[:, tg % 2, :], PS[:, 6 - tg % 2, :]).then_inc(s_xt, 1)
                def unit(n, tg):
                    o = tg % 2
                    for h in range(2):
                        act.wait_ge(s_up, 2 * n + h + 1)
                        if not (isinstance(n, int) and n < 2):
                            act.wait_ge(s_lo, 2 * (n - 1))
                        act.activation(h_f[:, o, h, :], PS[:, 2 * h:2 * h + 2, :].rearrange("p c t -> p (c t)"),
                                       ACT.Silu).then_inc(s_silu, 1)
                    if not (isinstance(n, int) and n < 2):
                        act.wait_ge(s_down, n - 1)
                    for h in range(2):
                        act.wait_ge(s_silu, 2 * n + h + 1)
                        act.copy(h_hi[:, o, h, :], h_f[:, o, h, :]).then_inc(s_hi, 1)

                unit(UNITS * m, 0)
                act.wait_ge(s_top, m + 1)
                act.activation(top_g[:, 1, :], top_g[:, 0, :], ACT.Exp).then_inc(s_e, 1)
                for tg in range(1, TG):
                    unit(UNITS * m + tg, tg)
                with act.Fori(0, NE) as e:
                    for tg in range(TG):
                        unit(UNITS * m + TG * (e + 1) + tg, tg)
                end_phase(act, phase)

            def attn_act():
                act.wait_ge(s_lnv, 3)
                act.activation(std[:, :], var[:, :], ACT.Sqrt).then_inc(s_std, 1)

                def columns(b, o):
                    act.wait_ge(s_xa_ps, b + 1)
                    act.copy(xa_t[:, o, :], PS[:, 5 * o, 0:T]).then_inc(s_xa_t, 1)

                def front_step(b, o, first, last):
                    if not last:
                        columns(b + 1, 1 - o)
                    for c in range(TB):
                        act.wait_ge(s_qkvm_ps, TB * b + c + 1)
                        act.copy(QKVM[:, ds(TB * b + c, 1), :].rearrange("p o n -> p (o n)"),
                                 PS[:, 1 + 5 * o + c, :]).then_inc(s_qkvm, 1)

                columns(0, 0)
                pipelined(act, front_step)
                act.wait_ge(s_ss, TB * B + 1)
                act.activation(rr[:, :, :], ss[:, :, :], ACT.Sqrt).then_inc(s_rs, 1)
                act.wait_ge(s_z0, 6)

                def banks(a):
                    return PS[:, a:a + 2, :].rearrange("p k (g t) -> p (k g) t", g=2)

                def keys(b, o, j0, j1):
                    act.wait_ge(s_kt_ps, b + 1)
                    for j in range(j0, j1):
                        lanes = slice(SLOT * j, SLOT * (j + 1))
                        act.copy(k_z[lanes, o, :, j, :], banks(0)[lanes, :, :]).then_inc(s_kz, 1)

                def queries(b):
                    act.wait_ge(s_qt_ps, b + 1)
                    act.copy(q_t[:, 0, :, :], banks(2)).then_inc(s_qt, 1)

                def outputs(b):
                    act.wait_ge(s_pv, NG * (b + 1))
                    wait(act, s_or_ps, b)
                    act.copy(o_t[:, :, :], banks(0)).then_inc(s_ot, 1)

                def step(b, o, first, last):
                    if not first:
                        outputs(b - 1)
                    if not last:
                        keys(b + 1, 1 - o, 0, 3)
                    act.wait_ge(s_qf_ps, 2 * b + 1)
                    act.copy(q_t[:, 1, 0:2, :], PS[:, 2, :].rearrange("p (g t) -> p g t", g=2)).then_inc(s_qf[0], 1)
                    if not last:
                        keys(b + 1, 1 - o, 3, 4)
                    for g_ in range(NG):
                        for c in range(TB):
                            i = TB * g_ + c
                            act.wait_ge(s_p2, 8 * b + i + 1)
                            wait(act, s_pv, NG * b + g_ - 1)
                            src = banks(4 + 2 * (i % 2))
                            dst = probs[:, g_ % 2, :, :]
                            act.activation(dst[:, :, T:T + P] if c else dst[:, :, 0:T], src[:, :, P:T] if c else src,
                                           ACT.Exp).then_inc(s_exp, 1)
                            if i == 6 and not last:
                                queries(b + 1)

                keys(0, 0, 0, 4)
                queries(0)
                pipelined(act, step)
                outputs(B - 1)
                end_phase(act, 4)

            moe_act(0, 2, 3)
            attn_act()
            moe_act(1, 4, 5)

        @block.tensor
        def _(pe):
            def front(b, o):
                pe.wait_ge(s_xn, TB * (b + 1))
                wait(pe, s_xn_t, b - 1)
                for c in range(TB):
                    m = pe.transpose(PS[:, 5 * o, c * P:(c + 1) * P], xn[:, o, c, :], ident[:, 0:P])
                m.then_inc(s_xn_ps, 1)
                pe.wait_ge(s_xn_t, b + 1)
                wait(pe, s_tap0, KI * (b - 1))
                for k in range(KI):
                    m = pe.matmul(PS[:, 1 + 5 * o, k * T:(k + 1) * T], w_in_s[:, k * P:(k + 1) * P], xn_t[:, o, :],
                                  start=True, stop=True)
                m.then_inc(s_xc_ps, 1)
                wait(pe, s_z, b - 1)
                for c in range(TB):
                    m = pe.matmul(PS[:, 2 + 5 * o, c * DI:(c + 1) * DI], xn_t[:, o, c * P:(c + 1) * P], w_in_s[:, DI:2 * DI],
                                  start=True, stop=True)
                m.then_inc(s_z_ps, 1)

            def front_step(b, o, first, last):
                if not last:
                    front(b + 1, 1 - o)
                pe.wait_ge(s_xs_t, KI * (b + 1))
                wait(pe, s_xr, TB * b)
                for c in range(TB):
                    for k in range(KI):
                        m = pe.matmul(PS[:, 3 + c, k * XRW:(k + 1) * XRW], xs_t[:, o, k, c * P:(c + 1) * P],
                                      idt_w[:, k, :], start=True, stop=True)
                m.then_inc(s_xr_ps, 1)

            pe.wait_ge(s_const, 4)
            pe.wait_ge(s_w_in, 16)
            front(0, 0)
            pe.wait_ge(s_const, 4 + KI)
            pe.wait_ge(s_w, W_ALL)
            pipelined(pe, front_step)

            def bc(b):
                for bank, w in ((0, b_w_s), (1, c_w_s)):
                    for q in range(KI):
                        for k in range(KI):
                            m = pe.matmul(PS[:, bank, q * T:(q + 1) * T], w[:, k, q * P:(q + 1) * P],
                                          XST[:, k, ds(b * T, T)], start=k == 0, stop=k == KI - 1)
                m.then_inc(s_bc_ps, 1)

            def scores(b, q):
                for r in range(2):
                    pe.matmul(PS[:, 2 + 3 * q, r * T:(r + 1) * T], b_t[:, q, 0:P], c_z[:, 2 * q + r, :],
                              start=True, stop=True)
                for r in range(2):
                    pe.matmul(PS[:, 3 + 3 * q, r * P:(r + 1) * P], b_t[:, q, P:T], c_z[:, 2 * q + r, P:T],
                              start=True, stop=True)
                for r in range(2):
                    for c in range(TB):
                        h = 2 * q + r
                        m = pe.transpose(PS[:, 4 + 3 * q, r * T + c * P:r * T + (c + 1) * P],
                                         ab_b[:, c, h:h + 1].broadcast_to((P, P)), ident[:, 0:P])
                m.then_inc(s_g_ps, 1)

            def y_rows(b):
                pe.wait_ge(s_wq, 2 * KI * (b + 1))
                pe.wait_ge(s_xdt, 2 * TB * (b + 1))
                for c in range(TB):
                    for h in range(NH):
                        q, r = h // 2, h % 2
                        o = PS[:, 2 + 3 * c, h * P:(h + 1) * P]
                        if c == 0:
                            m = pe.matmul(o, w0[:, q, r, 0:P], xdt[:, 0, q * P:(q + 1) * P], start=True, stop=True)
                        else:
                            pe.matmul(o, w0[:, q, r, P:T], xdt[:, 0, q * P:(q + 1) * P], start=True, stop=False)
                            m = pe.matmul(o, w1[:, q, r, :], xdt[:, 1, q * P:(q + 1) * P], start=False, stop=True)
                    m.then_inc(s_y_ps, 1)

            def project(b):
                pe.wait_ge(s_g, b + 1)
                pe.wait_ge(s_bc, 3 * (b + 1))
                for k in range(KI):
                    for c in range(TB):
                        m = pe.transpose(PS[:, 0, k * T + c * P:k * T + (c + 1) * P], g[:, c, k * P:(k + 1) * P],
                                         ident[:, 0:P])
                m.then_inc(s_gt_ps, 1)
                pe.wait_ge(s_gt, b + 1)
                for c in range(TB):
                    for k in range(KI):
                        m = pe.matmul(PS[:, 1, c * P:(c + 1) * P], g_t[:, k, c * P:(c + 1) * P], w_out_s[:, k, :],
                                      start=k == 0, stop=k == KI - 1)
                m.then_inc(s_o_ps, 1)

            def all_scores(b):
                pe.wait_ge(s_bc, 3 * (b + 1))
                pe.wait_ge(s_ab, b + 1)
                if not (isinstance(b, int) and b == 0):
                    pe.wait_ge(s_y, TB * b)
                for q in range(KI):
                    scores(b, q)

            pe.wait_ge(s_xst, B)
            pe.wait_ge(s_xn_t, B)
            pe.wait_ge(s_tap0, KI * B)
            bc(0)
            end_phase(pe, 1)
            all_scores(0)
            bc(1)
            y_rows(0)
            with pe.Fori(1, B - 1) as b:
                all_scores(b)
                project(b - 1)
                pe.wait_ge(s_o, b)
                bc(b + 1)
                y_rows(b)
            all_scores(B - 1)
            project(B - 2)
            y_rows(B - 1)
            pe.wait_ge(s_o, B - 1)
            project(B - 1)
            end_phase(pe, 2)

            def moe_pe(m, phase):
                pe.wait_ge(s_aw, 16 * 10)
                def columns(tg):
                    pe.wait_ge(s_xn4, TG * m + tg + 1)
                    wait(pe, s_xt, TG * m + tg - 1)
                    for i in range(GT):
                        mm = pe.transpose(PS[:, 6 - tg % 2, i * P:(i + 1) * P], xn4[:, tg % 2, i, :], ident[:, 0:P])
                    mm.then_inc(s_xt_ps, 1)

                columns(0)
                for tg in range(TG):
                    n = TG * m + tg
                    if tg < TG - 1:
                        columns(tg + 1)
                    pe.wait_ge(s_xt, n + 1)
                    wait(pe, s_lg, n - 1)
                    for i in range(GT):
                        mm = pe.matmul(PS[:, 7 - 3 * (tg % 2), i * NE:(i + 1) * NE], xt4[:, tg % 2, i * P:(i + 1) * P],
                                       gate_w_s[:, :], start=True, stop=True)
                    mm.then_inc(s_lg_ps, 1)

                def up(k, tg, o):
                    n = UNITS * m + TG * k + tg
                    if isinstance(k, int) and k == 0:
                        pe.wait_ge(s_xl, 2 * (TG * m + tg + 1))
                    if tg == 0:
                        pe.wait_ge(s_split, 2 * ((1 + NE) * m + k + 1))
                    cols = slice(tg * GN, (tg + 1) * GN)
                    for h in range(2):
                        if not (isinstance(n, int) and n == 0):
                            pe.wait_ge(s_silu, 2 * n + h - 1)
                        for c in (2 * h, 2 * h + 1):
                            hi, lo = (w[:, o, 0, c * P:(c + 1) * P] for w in (w_hi, w_lo))
                            pe.matmul(PS[:, c, :], hi, XH[:, cols], start=True, stop=False)
                            pe.matmul(PS[:, c, :], hi, XL[:, cols], start=False, stop=False)
                            mm = pe.matmul(PS[:, c, :], lo, XH[:, cols], start=False, stop=True)
                        mm.then_inc(s_up, 1)

                def down(k, tg, o):
                    n = UNITS * m + TG * k + tg
                    if not (isinstance(n, int) and n < 2):
                        pe.wait_ge(s_gated, n - 1)
                    bank = PS[:, 4 + tg % 2, :]
                    for h in range(2):
                        pe.wait_ge(s_lo, 2 * n + h + 1)
                        for i in range(2):
                            c = 2 * h + i
                            hi, lo = (w[:, o, 1, c * P:(c + 1) * P] for w in (w_hi, w_lo))
                            a_hi, a_lo = (a[:, tg % 2, h, i * GN:(i + 1) * GN] for a in (h_hi, h_lo))
                            pe.matmul(bank, hi, a_hi, start=c == 0, stop=False)
                            pe.matmul(bank, hi, a_lo, start=False, stop=False)
                            mm = pe.matmul(bank, lo, a_hi, start=False, stop=c == CH - 1)
                    mm.then_inc(s_down, 1)

                def back(tg):
                    pe.wait_ge(s_acc, UNITS * m + TG * NE + tg + 1)
                    if tg >= 2:
                        pe.wait_ge(s_res, TG * m + tg - 1)
                    for i in range(GT):
                        mm = pe.transpose(PS[:, 6 + tg % 2, i * P:(i + 1) * P], acc[:, tg * GN + i * P:tg * GN + (i + 1) * P],
                                          ident[:, 0:P])
                    mm.then_inc(s_acc_ps, 1)

                def expert(k, o, first=False, last=False):
                    for tg in range(TG):
                        if tg < TG - 1:
                            up(k, tg + 1, o)
                        elif not last:
                            up(k + 1, 0, 1 - o)
                        down(k, tg, o)
                        if first and tg == 1:
                            pe.wait_ge(s_gates, m + 1)
                            pe.transpose(PS[:, 7, 0:P], gates[:, :, :].rearrange("p e j -> p (e j)"),
                                         ident[:, 0:P]).then_inc(s_gates_ps, 1)
                        if last and tg >= 2:
                            back(tg - 2)

                up(0, 0, 0)
                pe.wait_ge(s_lg, TG * (m + 1))
                expert(0, 0, first=True)
                with pe.Fori(0, NE // 2 - 1) as i:
                    expert(2 * i + 1, 1)
                    expert(2 * i + 2, 0)
                expert(NE - 1, 1)
                expert(NE, 0, last=True)
                for tg in range(2, TG):
                    back(tg)
                end_phase(pe, phase)

            def attn_pe():
                pe.wait_ge(s_ac, 11)
                pe.wait_ge(s_aw, 16 * 10)
                pe.matmul(PS[0:HD, 7, 0:HD], w_dq_s[:, :], w_uq_s[:, :], start=True, stop=True)
                pe.matmul(PS[0:HD, 7, HD:2 * HD], w_dkv_s[:, :], w_ukv_s[:, 0:HD], start=True, stop=True)
                pe.matmul(PS[0:HD, 7, 3 * HD:4 * HD], w_kr_s[:, :], w_qr_s[:, :], start=True, stop=True)
                pe.matmul(PS[0:HD, 7, 4 * HD:5 * HD], w_ukv_s[:, HD:2 * HD], w_dkv_s[:, :], start=True, stop=True).then_inc(s_aw_ps, 1)
                pe.wait_ge(s_aw_c, 3)
                pe.matmul(PS[0:HD, 6, 0:HD], av[:, :], w_o_s[:, :], start=True, stop=True).then_inc(s_aw_ps, 1)
                pe.wait_ge(s_aw_c, 4)
                pe.matmul(PS[:, 7, 0:NSEC * HD], rep8[:, :, :].rearrange("e h f -> e (h f)"), small[:, :],
                          start=True, stop=True).then_inc(s_aw_ps, 1)

                def columns(b, o):
                    pe.wait_ge(s_xa, TB * (b + 1))
                    wait(pe, s_xa_t, b - 1)
                    for c in range(TB):
                        mm = pe.transpose(PS[:, 5 * o, c * P:(c + 1) * P], xa[:, o, c, :], ident[:, 0:P])
                    mm.then_inc(s_xa_ps, 1)

                def front_step(b, o, first, last):
                    if not last:
                        columns(b + 1, 1 - o)
                    pe.wait_ge(s_xa_t, b + 1)
                    if not first:
                        wait(pe, s_qkvm, TB * (b - 1))
                    for c in range(TB):
                        pe.matmul(PS[:, 1 + 5 * o + c, :], xa_t[:, o, c * P:(c + 1) * P],
                                  w_all[:, :, :, :].rearrange("p s h e -> p (s h e)"), start=True, stop=True).then_inc(s_qkvm_ps, 1)

                columns(0, 0)
                pe.wait_ge(s_wa, NSEC + 1)
                pipelined(pe, front_step)

                def to_columns(pad, bank, groups):
                    for g_ in groups:
                        for c in range(TB):
                            mm = pe.transpose(PS[:, bank + g_ // 2, (g_ % 2) * T + c * P:(g_ % 2) * T + (c + 1) * P],
                                              pad[:, c, 4 * g_:4 * g_ + 4, :].rearrange("p h s -> p (h s)"), ident[:, 0:P])
                    return mm

                def keys(b, o):
                    pe.wait_ge(s_kpad, 2 * (b + 1))
                    wait(pe, s_ot, b - 1)
                    to_columns(k_pad[:, o], 0, range(NG)).then_inc(s_kt_ps, 1)

                def queries(b, o):
                    pe.wait_ge(s_qpad, 2 * (b + 1))
                    pe.wait_ge(s_q1, 2 * (b + 1))
                    wait(pe, s_qf[0], b)
                    wait(pe, s_qf[1], b)
                    wait(pe, s_or, b - 1)
                    to_columns(q_pad[:, o], 2, range(NG)).then_inc(s_qt_ps, 1)

                def queries_less_max(b, o, half):
                    pe.wait_ge(s_nm, 4 * b + 2 * (half + 1))
                    to_columns(q_pad[:, o], 2, range(2 * half, 2 * half + 2)).then_inc(s_qf_ps, 1)

                def maxima(b, o, g_):
                    for c in range(TB):
                        i = TB * g_ + c
                        if i < 2:
                            wait(pe, s_exp, 8 * b + i - 1)
                        else:
                            pe.wait_ge(s_max, 8 * b + i - 1)
                        for j in range(4):
                            bank, at = 4 + 2 * (i % 2) + j // 2, (j % 2) * T
                            pe.matmul(PS[:, bank, at:at + T], q_t[:, 0, g_, c * P:(c + 1) * P], k_z[:, o, g_, j, :],
                                      start=True, stop=False)
                            mm = pe.matmul(PS[:, bank, at + c * P:at + (c + 1) * P], ident_b[:, :], mask_ts[:, :],
                                           start=False, stop=True)
                        mm.then_inc(s_p1, 1)

                def scores_less_max(b, o, i):
                    g_, c = i // TB, i % TB
                    if i < 2:
                        pe.wait_ge(s_max, 8 * b + 7 + i)
                    else:
                        pe.wait_ge(s_exp, 8 * b + i - 1)
                    for j in range(4):
                        bank, at = 4 + 2 * (i % 2) + j // 2, (j % 2) * T
                        pe.matmul(PS[:, bank, at:at + T], k_z[:, o, g_, j, c * P:(c + 1) * P], q_t[:, 1, g_, :],
                                  start=True, stop=False)
                        mm = pe.matmul(PS[:, bank, at + c * P:at + (c + 1) * P], ident_b[:, :], mask_st[:, :],
                                       start=False, stop=True)
                    mm.then_inc(s_p2, 1)

                def values(b, o, i):
                    g_, c = i // TB, i % TB
                    pe.wait_ge(s_exp, 8 * b + i + 1)
                    for j in range(4):
                        at = (g_ % 2) * T + c * P
                        mm = pe.matmul(PS[SLOT * j:SLOT * (j + 1), g_ // 2, at:(g_ % 2 + 1) * T],
                                       v_pad[:, o, c, 4 * g_ + j, :],
                                       probs[:, g_ % 2, j, T:T + P] if c else probs[:, g_ % 2, j, 0:T],
                                       start=c == 0, stop=c == 1, skip_group_check=True)
                    if c == 1:
                        mm.then_inc(s_pv, 1)

                def last_values(b, o):
                    for i in range(6, 8):
                        values(b, o, i)

                def output_rows(b):
                    pe.wait_ge(s_ot, b + 1)
                    wait(pe, s_or, b)
                    for c in range(TB):
                        for g_ in range(NG):
                            mm = pe.transpose(PS[:, 2 + c, g_ * P:(g_ + 1) * P], o_t[:, g_, c * P:(c + 1) * P], ident[:, 0:P])
                    mm.then_inc(s_or_ps, 1)

                def step(b, o, first, last):
                    pe.wait_ge(s_kz, 4 * (b + 1))
                    pe.wait_ge(s_qt, b + 1)
                    maxima(b, o, 0)
                    if not first:
                        last_values(b - 1, 1 - o)
                    maxima(b, o, 1)
                    if not last:
                        keys(b + 1, 1 - o)
                    maxima(b, o, 2)
                    queries_less_max(b, o, 0)
                    maxima(b, o, 3)
                    pe.wait_ge(s_qf[0], b + 1)
                    scores_less_max(b, o, 0)
                    scores_less_max(b, o, 1)
                    queries_less_max(b, o, 1)
                    scores_less_max(b, o, 2)
                    pe.wait_ge(s_v, b + 1)
                    pe.wait_ge(s_kz, 4 * (b + 1 if last else b + 2))
                    values(b, o, 0)
                    scores_less_max(b, o, 3)
                    values(b, o, 1)
                    pe.wait_ge(s_qf[1], b + 1)
                    if not first:
                        output_rows(b - 1)
                    scores_less_max(b, o, 4)
                    values(b, o, 2)
                    scores_less_max(b, o, 5)
                    values(b, o, 3)
                    if not last:
                        queries(b + 1, 1 - o)
                    for i in (6, 7):
                        scores_less_max(b, o, i)
                        values(b, o, i - 2)

                pe.wait_ge(s_z0, 6)
                keys(0, 0)
                queries(0, 0)
                pipelined(pe, step)
                last_values(B - 1, 1)
                output_rows(B - 1)
                end_phase(pe, 4)

            moe_pe(0, 3)
            attn_pe()
            moe_pe(1, 5)

        @block.vector
        def _(dve):
            def tile_stats(j0, n):
                for i in range(n):
                    dve.bn_stats(stats[:, ds(j0 + i, 1), :].rearrange("p o s -> p (o s)"),
                                 X[:, ds(j0 + i, 1), :].rearrange("p o s -> p (o s)"))

            def ln_finish(n):
                dve.drain()
                total, gap, squares, half = (mtmp[:, i, :] for i in range(4))
                dve.tensor_tensor(total, stats[:, :, 1], stats[:, :, 4], ALU.add)
                dve.tensor_tensor(gap, stats[:, :, 1], stats[:, :, 4], ALU.subtract)
                dve.tensor_tensor(squares, stats[:, :, 2], stats[:, :, 5], ALU.add)
                dve.drain()
                dve.tensor_scalar(mean[:, :], total, 0.5, None, ALU.mult)
                dve.scalar_tensor_tensor(half, gap, 0.25, gap, ALU.mult, ALU.mult)
                dve.tensor_scalar(squares, squares, 1.0 / D, LN_EPS, ALU.mult, ALU.add)
                dve.drain()
                dve.tensor_tensor(var[:, :], squares, half, ALU.add).then_inc(s_lnv, 1)
                dve.wait_ge(s_std, n)
                dve.reciprocal(rstd[:, :], std[:, :]).then_inc(s_ln, 1)
                dve.wait_ge(s_ln, n)

            dve.wait_ge(s_x, 16)
            with dve.Fori(0, TG) as tg:
                tile_stats(GT * tg, GT)
            ln_finish(1)

            def front(b, o):
                for c in range(TB):
                    j = TB * b + c
                    dve.tensor_scalar(xn[:, o, c, :], X[:, ds(j, 1), :].rearrange("p o d -> p (o d)"),
                                      mean[:, ds(j, 1)], rstd[:, ds(j, 1)],
                                      ALU.subtract, ALU.mult).then_inc(s_xn, 1)

            def front_step(b, o, first, last):
                if not last:
                    wait(dve, s_xn_ps, b)
                    front(b + 1, 1 - o)
                dve.wait_ge(s_xpad, b + 1)
                n = KI * (TAPS - 1) * b
                for t in range(TAPS - 1):
                    if t == 0:
                        dve.wait_ge(s_tap0, KI * (b + 1))
                    else:
                        dve.wait_ge(s_tap, n + KI * t)
                    for k in range(KI):
                        dve.scalar_tensor_tensor(conv_o[:, o, k, :], x_pad[:, o, k, t:t + T], conv_w_s[:, k, t:t + 1],
                                                 conv_o[:, o, k, :], ALU.mult, ALU.add).then_inc(s_tap, 1)
                if not first:
                    columns_copy(b - 1, 1 - o)

            def columns_copy(b, o):
                dve.wait_ge(s_xs_t, KI * (b + 1))
                dve.tensor_copy(XST[:, :, ds(b * T, T)], xs_t[:, o, :, :]).then_inc(s_xst, 1)

            front(0, 0)
            dve.wait_ge(s_w, W_ALL)
            pipelined(dve, front_step)
            columns_copy(B - 1, 1)
            v, nabs, u, w, lg, q = tmp
            dve.wait_ge(s_xr, TB * B)
            dve.tensor_tensor(v[:, :, :], XR[:, :, 0, P:XRW], XR[:, :, 1, P:XRW], ALU.add).then_inc(s_dtv, 1)
            dve.wait_ge(s_dtv, 1)
            dve.tensor_tensor(v[:, :, :], v[:, :, :], row_nh[:, 1:2, :].broadcast_to((P, NT, NH)), ALU.add).then_inc(s_dtv, 1)
            dve.wait_ge(s_dtv, 2)
            dve.scalar_tensor_tensor(nabs[:, :, :], v[:, :, :], -1.0, v[:, :, :], ALU.mult, ALU.min).then_inc(s_dtv, 1)
            dve.wait_ge(s_dta, 1)
            dve.tensor_scalar(w[:, :, :], u[:, :, :], 1.0, None, ALU.add).then_inc(s_dtv, 1)
            dve.wait_ge(s_dtv, 4)
            dve.tensor_scalar(q[:, :, :], w[:, :, :], -1.0, 0.0, ALU.add, ALU.is_equal).then_inc(s_dtv, 1)
            dve.wait_ge(s_dtv, 5)
            dve.wait_ge(s_dta, 3)
            dve.scalar_tensor_tensor(w[:, :, :], w[:, :, :], -1.0, q[:, :, :], ALU.add, ALU.add).then_inc(s_dtv, 1)
            dve.tensor_tensor(lg[:, :, :], lg[:, :, :], q[:, :, :], ALU.add).then_inc(s_dtv, 1)
            dve.wait_ge(s_dtv, 7)
            dve.reciprocal(nabs[:, :, :], w[:, :, :]).then_inc(s_dtv, 1)
            dve.tensor_tensor(lg[:, :, :], lg[:, :, :], u[:, :, :], ALU.mult).then_inc(s_dtv, 1)
            dve.wait_ge(s_dtv, 9)
            dve.tensor_tensor(lg[:, :, :], lg[:, :, :], nabs[:, :, :], ALU.mult).then_inc(s_dtv, 1)
            dve.wait_ge(s_dtv, 10)
            dve.scalar_tensor_tensor(DT[:, :, :], v[:, :, :], 0.0, lg[:, :, :], ALU.max, ALU.add).then_inc(s_dtv, 1)
            dve.wait_ge(s_dtv, 11)
            dve.wait_ge(s_dta, 2)
            dve.tensor_tensor(nabs[:, :, :], DT[:, :, :], neg_a[:, :].unsqueeze(1).broadcast_to((P, NT, NH)),
                              ALU.mult).then_inc(s_dtv, 1)
            end_phase(dve, 1)

            def decays(b, q):
                dve.wait_ge(s_g_ps, KI * b + q + 1)
                if not (isinstance(b, int) and b == 0):
                    dve.wait_ge(s_wq, 2 * KI * (b - 1) + 2 * (q + 1))
                for r in range(2):
                    dve.tensor_tensor_scan(dec0[:, q, r, :], PS[:, 4 + 3 * q, r * T:(r + 1) * T], ident[:, :], 0.0,
                                           ALU.mult, ALU.add).then_inc(s_dec, 1)
                    dve.tensor_tensor_scan(dec1[:, q, r, :], PS[:, 4 + 3 * q, r * T + P:(r + 1) * T], ident[:, 0:P], 0.0,
                                           ALU.mult, ALU.add).then_inc(s_dec, 1)
                dve.wait_ge(s_dec, 4 * (KI * b + q + 1))
                dve.tensor_tensor(w0[:, q, :, :], dec0[:, q, :, :], PS[:, 2 + 3 * q, :].rearrange("p (r t) -> p r t", r=2),
                                  ALU.mult).then_inc(s_wq, 1)
                dve.tensor_tensor(w1[:, q, :, :], dec1[:, q, :, :],
                                  PS[:, 3 + 3 * q, 0:2 * P].rearrange("p (r t) -> p r t", r=2),
                                  ALU.mult).then_inc(s_wq, 1)

            def y_norm(b):
                if not (isinstance(b, int) and b == 0):
                    dve.wait_ge(s_yn, b)
                for c in range(TB):
                    dve.wait_ge(s_y_ps, TB * b + c + 1)
                    for q in range(KI):
                        own = PS[:, 2 + 3 * c, q * T:(q + 1) * T].rearrange("p (r e) -> p r e", r=4)[:, 0:4:3, :]
                        m = dve.tensor_tensor(y[:, c, q * P:(q + 1) * P].rearrange("p (r e) -> p r e", r=2), own,
                                              dx[:, c, q * P:(q + 1) * P].rearrange("p (r e) -> p r e", r=2), ALU.add)
                    m.then_inc(s_y, 1)
                for c in range(TB):
                    dve.wait_ge(s_y, TB * b + c + 1)
                    dve.bn_stats(yst[:, c, :], y[:, c, :])
                dve.drain()
                for c in range(TB):
                    dve.bn_aggr(ymv[:, c, :], yst[:, c, :]).then_inc(s_ymv, 1)
                dve.wait_ge(s_ysd, b + 1)
                dve.reciprocal(yrs[:, :], ysd[:, :]).then_inc(s_yrs, 1)
                dve.wait_ge(s_yrs, b + 1)
                wait(dve, s_yw, b)
                for c in range(TB):
                    m = dve.tensor_scalar(yn[:, c, :], y[:, c, :], ymv[:, c, 0:1], yrs[:, c:c + 1], ALU.subtract, ALU.mult)
                m.then_inc(s_yn, 1)

            def residual(b):
                dve.wait_ge(s_o_ps, b + 1)
                rows = X[:, ds(TB * b, TB), :]
                dve.tensor_tensor(rows, PS[:, 1, 0:T].rearrange("p (c d) -> p c d", c=TB), rows, ALU.add).then_inc(s_o, 1)

            for q in range(KI):
                decays(0, q)
            y_norm(0)
            with dve.Fori(1, B) as b:
                for q in range(KI):
                    decays(b, q)
                residual(b - 1)
                y_norm(b)
                dve.wait_ge(s_o, b)
                tile_stats(TB * (b - 1), TB)
            residual(B - 1)
            dve.wait_ge(s_o, B)
            tile_stats(TB * (B - 1), TB)
            end_phase(dve, 2)

            def normalise(dst, j):
                return dve.tensor_scalar(dst, X[:, ds(j, 1), :].rearrange("p o d -> p (o d)"), mean[:, ds(j, 1)],
                                         rstd[:, ds(j, 1)], ALU.subtract, ALU.mult)

            def best(m):
                for j in range(NT):
                    dve.max(top[:, j, :], logits[:, j, :])
                dve.drain()
                dve.tensor_tensor(top_g[:, 0, :], top[:, :, 1], top[:, :, 0], ALU.subtract).then_inc(s_top, 1)

            def which(m):
                for j in range(NT):
                    dve.max_index(top_i[:, j, :], top[:, j, :], logits[:, j, :])
                dve.wait_ge(s_e, m + 1)
                dve.tensor_scalar(top_g[:, 2, :], top_g[:, 1, :], 1.0, None, ALU.add)
                dve.drain()
                dve.tensor_copy(top_if[:, :, :], top_i[:, :, 0:2])
                dve.reciprocal(top_g[:, 3, :], top_g[:, 2, :])
                dve.drain()
                dve.tensor_tensor(top_g[:, 2, :], top_g[:, 1, :], top_g[:, 3, :], ALU.mult)
                for i in range(2):
                    dve.tensor_tensor(pick[:, i, :, :], iota[:, :].unsqueeze(1).broadcast_to((P, NT, NE)),
                                      top_if[:, :, i:i + 1].broadcast_to((P, NT, NE)), ALU.is_equal)
                dve.drain()
                for i in range(2):
                    dve.tensor_tensor(pick[:, i, :, :], pick[:, i, :, :],
                                      top_g[:, 3 - i, :].unsqueeze(2).broadcast_to((P, NT, NE)), ALU.mult)
                dve.drain()
                dve.tensor_tensor(gates[:, :, :].rearrange("p e j -> p j e"), pick[:, 0, :, :], pick[:, 1, :, :],
                                  ALU.add).then_inc(s_gates, 1)

            def gates_columns(m):
                dve.wait_ge(s_gates_ps, m + 1)
                dve.tensor_copy(gates_t[:, :], PS[:, 7, 0:P]).then_inc(s_gates_t, 1)

            def moe_dve(m, ln, phase):
                ln_finish(ln)

                def norm4(tg):
                    wait(dve, s_xt_ps, TG * m + tg - 1)
                    for i in range(GT):
                        mm = normalise(xn4[:, tg % 2, i, :], GT * tg + i)
                    mm.then_inc(s_xn4, 1)

                norm4(0)
                norm4(1)
                for tg in range(TG):
                    n = TG * m + tg
                    cols = slice(GN * tg, GN * (tg + 1))
                    dve.wait_ge(s_xt, n + 1)
                    dve.tensor_copy(XH[:, cols], xt4[:, tg % 2, :]).then_inc(s_xl, 1)
                    if tg + 2 < TG:
                        norm4(tg + 2)
                    dve.wait_ge(s_xl, 2 * n + 1)
                    dve.tensor_tensor(XL[:, cols], xt4[:, tg % 2, :], XH[:, cols].bitcast(F32), ALU.subtract).then_inc(s_xl, 1)
                    dve.wait_ge(s_lg_ps, n + 1)
                    dve.tensor_copy(logits[:, GT * tg:GT * (tg + 1), :].rearrange("p j e -> p (j e)"),
                                    PS[:, 7 - 3 * (tg % 2), 0:GT * NE]).then_inc(s_lg, 1)
                dve.wait_ge(s_lg, TG * (m + 1))

                def low(n, tg):
                    o = tg % 2
                    if not (isinstance(n, int) and n < 2):
                        dve.wait_ge(s_down, n - 1)
                    for h in range(2):
                        dve.wait_ge(s_hi, 2 * n + h + 1)
                        dve.tensor_tensor(h_lo[:, o, h, :], h_f[:, o, h, :], h_hi[:, o, h, :].bitcast(F32),
                                          ALU.subtract).then_inc(s_lo, 1)

                def gate(k, tg, o=None, i=None):
                    n = UNITS * m + TG * k + tg
                    dve.wait_ge(s_down, n + 1)
                    cols = slice(tg * GN, (tg + 1) * GN)
                    if not (isinstance(n, int) and n < 2):
                        dve.wait_ge(s_acc, n - 1)
                    if o is None:
                        dve.tensor_copy(gy[:, tg % 2, :], PS[:, 4 + tg % 2, :]).then_inc(s_gated, 1)
                        return
                    if tg == 0:
                        dve.wait_ge(s_gb[o], 16 * (NE // 2 * m + i + 1))
                    dve.tensor_tensor(gy[:, tg % 2, :], gates_b[:, o, cols], PS[:, 4 + tg % 2, :], ALU.mult).then_inc(s_gated, 1)

                def residual(tg):
                    dve.wait_ge(s_acc_ps, TG * m + tg + 1)
                    rows = X[:, GT * tg:GT * (tg + 1), :]
                    dve.tensor_tensor(rows, PS[:, 6 + tg % 2, :].rearrange("p (i d) -> p i d", i=GT), rows,
                                      ALU.add).then_inc(s_res, 1)

                def next_stats(tg):
                    if ln < LAST_LN:
                        dve.wait_ge(s_res, TG * m + tg + 1)
                        tile_stats(GT * tg, GT)

                low(UNITS * m, 0)
                best(m)
                low(UNITS * m + 1, 1)
                gate(0, 0)
                which(m)
                low(UNITS * m + 2, 2)
                gate(0, 1)
                gates_columns(m)
                low(UNITS * m + 3, 3)
                gate(0, 2)
                low(UNITS * m + TG, 0)
                gate(0, TG - 1)
                with dve.Fori(0, NE // 2 - 1) as i:
                    for o in range(2):
                        k = 2 * i + 1 + o
                        for tg in range(TG):
                            low(UNITS * m + TG * k + tg + 1, (tg + 1) % TG)
                            gate(k, tg, o, i)
                for o in range(2):
                    k = NE - 1 + o
                    for tg in range(TG):
                        if k < NE or tg < TG - 1:
                            low(UNITS * m + TG * k + tg + 1, (tg + 1) % TG)
                        gate(k, tg, o, NE // 2 - 1)
                        if k == NE and tg >= 2:
                            residual(tg - 2)
                for tg in range(TG):
                    if tg >= 2:
                        residual(tg)
                    next_stats(tg)
                end_phase(dve, phase)

            def attn_dve():
                dve.wait_ge(s_aw, 16 * 10)
                dve.wait_ge(s_ac, 11)
                dve.wait_ge(s_aw_ps, 1)
                dve.tensor_copy(small[:, 0:2 * HD], PS[0:HD, 7, 0:2 * HD]).then_inc(s_aw_c, 1)
                dve.scalar_tensor_tensor(small[:, 3 * HD:4 * HD], PS[0:HD, 7, 3 * HD:4 * HD], HD ** -0.5,
                                         row_qk[0:HD, 0, :], ALU.mult, ALU.mult).then_inc(s_aw_c, 1)
                dve.tensor_copy(av[:, :], PS[0:HD, 7, 4 * HD:5 * HD]).then_inc(s_aw_c, 1)
                dve.wait_ge(s_aw_ps, 2)
                dve.tensor_copy(small[:, 2 * HD:3 * HD], PS[0:HD, 6, 0:HD]).then_inc(s_aw_c, 1)
                dve.scalar_tensor_tensor(row_qk[:, 2, :], row_qk[:, 0, :], HD ** -0.5, row_qk[:, 1, :], ALU.mult,
                                         ALU.mult).then_inc(s_wa, 1)
                dve.wait_ge(s_aw_ps, 3)
                dve.tensor_copy(wa_rep[:, :], PS[:, 7, 0:NSEC * HD])
                dve.drain()
                for i in range(NSEC):
                    dve.tensor_tensor(w_all[:, i, :, :], wa_rep[:, i * HD:(i + 1) * HD].unsqueeze(1).broadcast_to((P, H, HD)),
                                      head_of[:, :].unsqueeze(2).broadcast_to((P, H, HD)), ALU.mult).then_inc(s_wa, 1)
                ln_finish(3)

                def front(b, o):
                    wait(dve, s_xa_ps, b - 1)
                    for c in range(TB):
                        normalise(xa[:, o, c, :], TB * b + c).then_inc(s_xa, 1)

                def square_sums(b, o):
                    for c in range(TB):
                        dve.wait_ge(s_sq, TB * b + c + 1)
                        dve.tensor_reduce(ss[:, ds(TB * b + c, 1), :].rearrange("p o h -> p (o h)"),
                                          sq[:, o, c, :].rearrange("p (h e) -> p h e", e=HD), AX.X, ALU.add).then_inc(s_ss, 1)

                def front_step(b, o, first, last):
                    if not last:
                        front(b + 1, 1 - o)
                    if not first:
                        square_sums(b - 1, 1 - o)

                front(0, 0)
                pipelined(dve, front_step)
                square_sums(B - 1, 1)
                dve.drain()
                dve.tensor_scalar(ss[:, :, :], ss[:, :, :], 1.0 / HD, RMS_EPS, ALU.mult, ALU.add).then_inc(s_ss, 1)
                dve.wait_ge(s_rs, 1)
                dve.reciprocal(rr[:, 0:TB, :], rr[:, 0:TB, :]).then_inc(s_rr, 1)
                dve.reciprocal(rr[:, TB:, :], rr[:, TB:, :]).then_inc(s_rr, 1)

                def flat(t):
                    return t.rearrange("p c (h e) -> p (c h) e", h=H)

                def maxima(b, g_):
                    for c in range(TB):
                        i = TB * g_ + c
                        dve.wait_ge(s_p1, 8 * b + i + 1)
                        scores = PS[:, 4 + 2 * (i % 2):6 + 2 * (i % 2), :].rearrange("p k (j t) -> p (k j) t", j=2)
                        dve.tensor_reduce(neg_max[:, c, 4 * g_:4 * g_ + 4], scores[:, :, 0:(c + 1) * P], AX.X, ALU.max,
                                          negate=True).then_inc(s_max, 1)

                def place(b, o, half):
                    dve.wait_ge(s_max, 8 * b + 4 * (half + 1))
                    heads = slice(8 * half, 8 * (half + 1))
                    nm = neg_max[:, :, heads]
                    nm_hi, nm_lo = (q_pad[:, o, :, heads, 3 * HD + a] for a in range(2))
                    dve.tensor_copy(nm_hi.bitcast(F32R), nm).then_inc(s_nm, 1)
                    dve.wait_ge(s_nm, 4 * b + 2 * half + 1)
                    dve.tensor_tensor(nm_lo.bitcast(F32R), nm, nm_hi, ALU.subtract).then_inc(s_nm, 1)

                def finish(b):
                    dve.wait_ge(s_or_ps, b + 1)
                    rows = PS[:, 2:4, :].rearrange("p c (h s) -> p c h s", s=SLOT)
                    dve.reciprocal(den[:, :, :], rows[:, :, :, HD]).then_inc(s_den, 1)
                    dve.wait_ge(s_den, b + 1)
                    dve.tensor_tensor(flat(o_r[:, :, :]), rows[:, :, :, 0:HD].rearrange("p c h e -> p (c h) e"),
                                      den[:, :, :].rearrange("p c (h o) -> p (c h) o", o=1).broadcast_to((P, TB * H, HD)),
                                      ALU.mult).then_inc(s_or, 1)
                    dve.wait_ge(s_or, b + 1)
                    rows = X[:, ds(TB * b, TB), :]
                    dve.tensor_tensor(rows, rows, o_r[:, :, :], ALU.add).then_inc(s_res_a, 1)

                def next_stats(b):
                    dve.wait_ge(s_res_a, b + 1)
                    tile_stats(TB * b, TB)

                def step(b, o, first, last):
                    wait(dve, s_nm, 4 * b)
                    maxima(b, 0)
                    maxima(b, 1)
                    place(b, o, 0)
                    maxima(b, 2)
                    maxima(b, 3)
                    place(b, o, 1)
                    dve.wait_ge(s_qf_ps, 2 * b + 2)
                    dve.tensor_copy(q_t[:, 1, 2:4, :], PS[:, 3, :].rearrange("p (g t) -> p g t", g=2)).then_inc(s_qf[1], 1)
                    if not first:
                        wait(dve, s_res_a, b - 1)
                        finish(b - 1)
                        next_stats(b - 1)

                pipelined(dve, step)
                finish(B - 1)
                next_stats(B - 1)
                end_phase(dve, 4)

            moe_dve(0, 2, 3)
            attn_dve()
            moe_dve(1, 4, 5)


_INPUTS = ("x", "w_in", "conv_w", "conv_b", "a_log", "dt_w", "dt_b", "b_w", "c_w", "d_skip", "ln_w", "ln_b", "w_out",
           "w_dq", "w_uq_t", "w_dkv", "w_ukv_t", "w_qr", "w_kr", "w_o_t", "qn_w", "kn_w", "moe_w1", "moe_w2", "gate_w")


def kernel(**inputs):
    import numpy as np
    import concourse.bacc as bacc
    from concourse.bass_utils import run_bass_kernel_spmd as run

    i = {k: np.asarray(v) for k, v in inputs.items()}
    a, m, f = ({k[len(p):]: v for k, v in i.items() if k.startswith(p)} for p in ("L0_attn_a_", "L0_attn_b_", "L0_ffn_"))
    x = a["hidden_states"]
    by_chunk = lambda w: w.T.reshape(2, 128, -1).transpose(1, 0, 2)
    arrays = dict(
        x=x.reshape(-1, x.shape[-1]), w_in=a["in_proj_w"].T,
        conv_w=a["conv_w"].reshape(2, 128, -1).transpose(1, 0, 2), conv_b=a["conv_b"].reshape(2, 128).T,
        a_log=a["A_log"][None], dt_w=by_chunk(a["dt_w"]), dt_b=a["dt_b"][None],
        b_w=by_chunk(a["B_w"]), c_w=by_chunk(a["C_w"]), d_skip=a["D"][None], ln_w=a["ln_w"][None], ln_b=a["ln_b"][None],
        w_out=a["out_proj_w"].T.reshape(2, 128, -1),
        w_dq=m["W_DQ"], w_uq_t=m["W_UQ"].T, w_dkv=m["W_DKV"], w_ukv_t=m["W_UKV"].T, w_qr=m["W_QR"], w_kr=m["W_KR"],
        w_o_t=m["W_O"].T, qn_w=m["q_norm_w"][None], kn_w=m["k_norm_w"][None],
        moe_w1=np.concatenate([f["shared_w1"][None], f["experts_w1"]]).transpose(0, 2, 1),
        moe_w2=np.concatenate([f["shared_w2"][None], f["experts_w2"]]).transpose(0, 2, 1).reshape(9, 4, 128, 128).transpose(0, 2, 1, 3),
        gate_w=f["gate_w"].T,
    )
    arrays = {k: np.ascontiguousarray(arrays[k]) for k in _INPUTS}
    nc = bacc.Bacc("TRN2", target_bir_lowering=False, num_devices=1)
    args = [nc.dram_tensor(k, arrays[k].shape, mybir.dt.from_np(arrays[k].dtype), kind="ExternalInput").ap() for k in _INPUTS]
    o = nc.dram_tensor("out", arrays["x"].shape, F32, kind="ExternalOutput").ap()
    hybrid_kernel(nc, *args, o)
    r = run(nc, [arrays], core_ids=[0])
    return np.asarray(r.results[0]["out"]).reshape(x.shape)
```

```python
from contextlib import ExitStack

import concourse.bass as bass
from concourse import mybir

F32 = mybir.dt.float32
F32R = mybir.dt.float32r
BF16 = mybir.dt.bfloat16
U32 = mybir.dt.uint32
ALU = mybir.AluOpType
ACT = mybir.ActivationFunctionType
AX = mybir.AxisListType
ds = bass.ds

P = 128
LN_EPS = 1e-5
RMS_EPS = 1.1920929e-07
MASKED = -1e30


def hybrid_kernel(nc, x, w_in, conv_w, conv_b, a_log, dt_w, dt_b, b_w, c_w, d_skip, ln_w, ln_b, w_out,
                  w_dq, w_uq_t, w_dkv, w_ukv_t, w_qr, w_kr, w_o_t, qn_w, kn_w,
                  moe_w1, moe_w2, gate_w, out):
    B, T, D = 8, 256, x.shape[1]
    NT = x.shape[0] // P
    TB = T // P
    DI = w_out.shape[0] * w_out.shape[1]
    KI = DI // P
    NH = a_log.shape[1]
    HP = DI // NH
    TAPS = conv_w.shape[2]
    H = 16
    HD = D // H
    NG = H // 4
    NE = gate_w.shape[1]
    HID = moe_w1.shape[2]
    CH = HID // P
    TG = 4
    GT = NT // TG
    GN = GT * P
    XRW = P + NH
    assert B * TB == NT and KI == 2 and NH == 4 and TB == 2 and NE == 8 and CH == 4

    with ExitStack() as ctx:
        def sb(name, shape, dt=F32, stack=ctx):
            return stack.enter_context(nc.sbuf_tensor(name, shape, dt))

        def sem(name):
            return ctx.enter_context(nc.semaphore(name))

        PS = ctx.enter_context(nc.psum_tensor("PS", [P, 8, 512], F32))

        X = sb("X", [P, NT, D])
        ident = sb("ident", [P, 2 * P])
        stats = sb("stats", [P, NT, 6])
        mean = sb("mean", [P, NT])
        var = sb("var", [P, NT])
        mtmp = sb("mtmp", [P, 4, NT])
        rstd = sb("rstd", [P, NT])
        std = sb("std", [P, NT])
        xn4 = sb("xn4", [P, 2, GT, D])
        xt4 = sb("xt4", [P, 2, GN])

        raw = sb("raw", [P, 2, HID])
        w_hi = sb("w_hi", [P, 2, 2, HID], F32R)
        w_lo = sb("w_lo", [P, 2, 2, HID], F32R)
        gate_w_s = sb("gate_w_s", [P, NE])
        iota = sb("iota", [P, NE])
        iota_i = sb("iota_i", [P, NE], mybir.dt.int32)
        NSEC = 4
        SLOT = 32
        w_dq_s = sb("w_dq_s", [64, HD]); w_uq_s = sb("w_uq_s", [64, HD])
        w_dkv_s = sb("w_dkv_s", [P, HD]); w_ukv_s = sb("w_ukv_s", [P, 2 * HD])
        w_qr_s = sb("w_qr_s", [64, HD]); w_kr_s = sb("w_kr_s", [64, HD]); w_o_s = sb("w_o_s", [HD, HD])
        row_qk = sb("row_qk", [P, 3, HD])
        small = sb("small", [HD, NSEC * HD])
        av = sb("av", [HD, HD])
        rep8 = sb("rep8", [HD, H, HD])
        wa_rep = sb("wa_rep", [P, NSEC * HD])
        head_of = sb("head_of", [P, H])
        w_all = sb("w_all", [P, NSEC, H, HD])
        ident_b = sb("ident_b", [P, P], BF16)
        mask_ts = sb("mask_ts", [P, 2, P], BF16)
        mask_st = sb("mask_st", [P, 2, P], BF16)

        mamba = ExitStack()
        w_in_s = sb("w_in_s", [P, 2 * DI], stack=mamba)
        conv_w_s = sb("conv_w_s", [P, KI, TAPS], stack=mamba)
        conv_b_s = sb("conv_b_s", [P, KI], stack=mamba)
        idt_w = sb("idt_w", [P, KI, XRW], stack=mamba)
        b_w_s = sb("b_w_s", [P, KI, DI], stack=mamba)
        c_w_s = sb("c_w_s", [P, KI, DI], stack=mamba)
        w_out_s = sb("w_out_s", [P, KI, D], stack=mamba)
        row_nh = sb("row_nh", [P, 3, NH], stack=mamba)
        row_ln = sb("row_ln", [P, 2, DI], stack=mamba)
        neg_a = sb("neg_a", [P, NH], stack=mamba)
        xn = sb("xn", [P, 2, TB, D], stack=mamba)
        xn_t = sb("xn_t", [P, 2, T], stack=mamba)
        x_pad = sb("x_pad", [P, 2, KI, TAPS - 1 + T], stack=mamba)
        conv_o = sb("conv_o", [P, 2, KI, T], stack=mamba)
        xs_t = sb("xs_t", [P, 2, KI, T], stack=mamba)
        z_act = sb("z_act", [P, 2, TB, DI], stack=mamba)
        XST = sb("XST", [P, KI, B * T], stack=mamba)
        XR = sb("XR", [P, NT, KI, XRW], stack=mamba)
        ZW = sb("ZW", [P, NT, DI], stack=mamba)
        ZB = sb("ZB", [P, NT, DI], stack=mamba)
        DT = sb("DT", [P, NT, NH], stack=mamba)
        AB = sb("AB", [P, NT, NH], stack=mamba)
        tmp = [sb(f"dt_tmp{i}", [P, NT, NH], stack=mamba) for i in range(6)]
        b_t = sb("b_t", [P, KI, T], stack=mamba)
        c_z = sb("c_z", [P, NH, T], stack=mamba)
        ab_b = sb("ab_b", [P, 2, TB, NH], stack=mamba)
        xdt = sb("xdt", [P, 2, TB, DI], stack=mamba)
        dx = sb("dx", [P, 2, TB, DI], stack=mamba)
        dec0 = sb("dec0", [P, KI, 2, T], stack=mamba)
        dec1 = sb("dec1", [P, KI, 2, P], stack=mamba)
        w0 = sb("w0", [P, KI, 2, T], stack=mamba)
        w1 = sb("w1", [P, KI, 2, P], stack=mamba)
        y = sb("y", [P, TB, DI], stack=mamba)
        yst = sb("yst", [P, TB, 6], stack=mamba)
        ymv = sb("ymv", [P, TB, 2], stack=mamba)
        ysd = sb("ysd", [P, TB], stack=mamba)
        yrs = sb("yrs", [P, TB], stack=mamba)
        yn = sb("yn", [P, TB, DI], stack=mamba)
        yw = sb("yw", [P, TB, DI], stack=mamba)
        g = sb("g", [P, TB, DI], stack=mamba)
        g_t = sb("g_t", [P, KI, T], stack=mamba)
        mamba.close()

        moe = ExitStack()
        XH = sb("XH", [P, NT * P], F32R, stack=moe)
        XL = sb("XL", [P, NT * P], F32R, stack=moe)
        acc = sb("acc", [P, NT * P], stack=moe)
        h_f = sb("h_f", [P, 2, 2, 2 * GN], stack=moe)
        h_hi = sb("h_hi", [P, 2, 2, 2 * GN], F32R, stack=moe)
        h_lo = sb("h_lo", [P, 2, 2, 2 * GN], F32R, stack=moe)
        gates_b = sb("gates_b", [P, 2, NT * P], stack=moe)
        gy = sb("gy", [P, 2, GN], stack=moe)
        logits = sb("logits", [P, NT, NE], stack=moe)
        top = sb("top", [P, NT, 8], stack=moe)
        top_i = sb("top_i", [P, NT, 8], U32, stack=moe)
        top_if = sb("top_if", [P, NT, 2], stack=moe)
        top_g = sb("top_g", [P, 4, NT], stack=moe)
        pick = sb("pick", [P, 2, NT, NE], stack=moe)
        gates = sb("gates", [P, NE, NT], stack=moe)
        gates_t = sb("gates_t", [P, P], stack=moe)
        moe.close()
        gates_d = nc.dram_tensor("gates_d", (P, P), F32).ap()

        attn = ExitStack()
        QKVM = sb("QKVM", [P, NT, NSEC * D], stack=attn)
        xa = sb("xa", [P, 2, TB, D], stack=attn)
        xa_t = sb("xa_t", [P, 2, T], stack=attn)
        sq = sb("sq", [P, 2, TB, 2 * D], stack=attn)
        ss = sb("ss", [P, NT, 2 * H], stack=attn)
        rr = sb("rr", [P, NT, 2 * H], stack=attn)
        q1 = sb("q1", [P, TB, D], stack=attn)
        kn = sb("kn", [P, 3, TB, D], stack=attn)
        q_pad = sb("q_pad", [P, 2, TB, H, SLOT], stack=attn)
        k_pad = sb("k_pad", [P, 2, TB, H, SLOT], stack=attn)
        v_pad = sb("v_pad", [P, 2, TB, H, SLOT], stack=attn)
        q_t = sb("q_t", [P, 2, NG, T], F32R, stack=attn)
        k_z = sb("k_z", [P, 2, NG, 4, T], F32R, stack=attn)
        neg_max = sb("neg_max", [P, TB, H], stack=attn)
        probs = sb("probs", [P, 2, 4, T + P], stack=attn)
        o_t = sb("o_t", [P, NG, T], stack=attn)
        den = sb("den", [P, TB, H], stack=attn)
        o_r = sb("o_r", [P, TB, D], stack=attn)
        attn.close()

        s_x = [sem(f"s_x{i}") for i in range(TG)]; s_w = sem("s_w"); s_w_in = sem("s_w_in")
        s_w_conv = sem("s_w_conv"); s_tap0 = sem("s_tap0"); s_const = sem("s_const"); s_out = sem("s_out")
        s_phase = sem("s_phase")
        s_ln = sem("s_ln"); s_lnv = sem("s_lnv"); s_std = sem("s_std")
        s_xn = sem("s_xn"); s_xn_ps = sem("s_xn_ps"); s_xn_t = sem("s_xn_t")
        s_xc_ps = sem("s_xc_ps"); s_z_ps = sem("s_z_ps"); s_xpad = sem("s_xpad"); s_z = sem("s_z")
        s_zw = sem("s_zw"); s_tap = sem("s_tap"); s_xs_t = sem("s_xs_t"); s_xst = sem("s_xst")
        s_xr_ps = sem("s_xr_ps"); s_xr = sem("s_xr")
        s_dtv = sem("s_dtv"); s_dta = sem("s_dta")
        s_bc_ps = sem("s_bc_ps"); s_bc = sem("s_bc"); s_ab = sem("s_ab"); s_xdt = sem("s_xdt")
        s_g_ps = sem("s_g_ps"); s_dec = sem("s_dec"); s_wq = sem("s_wq")
        s_y_ps = sem("s_y_ps"); s_y = sem("s_y"); s_ymv = sem("s_ymv")
        s_ysd = sem("s_ysd"); s_yrs = sem("s_yrs"); s_yn = sem("s_yn"); s_yw = sem("s_yw"); s_g = sem("s_g")
        s_gt_ps = sem("s_gt_ps"); s_gt = sem("s_gt"); s_o_ps = sem("s_o_ps"); s_o = sem("s_o")

        s_raw = sem("s_raw"); s_split = sem("s_split"); s_xn4 = sem("s_xn4"); s_xt_ps = sem("s_xt_ps")
        s_xt = sem("s_xt"); s_xl = sem("s_xl"); s_lg_ps = sem("s_lg_ps"); s_lg = sem("s_lg")
        s_top = sem("s_top"); s_e = sem("s_e"); s_gates = sem("s_gates"); s_gates_ps = sem("s_gates_ps")
        s_gates_t = sem("s_gates_t"); s_gates_d = sem("s_gates_d"); s_gb = [sem(f"s_gb{i}") for i in range(2)]
        s_up = sem("s_up"); s_silu = sem("s_silu"); s_hi = sem("s_hi"); s_lo = sem("s_lo")
        s_down = sem("s_down"); s_gated = sem("s_gated"); s_acc = sem("s_acc")
        s_acc_ps = sem("s_acc_ps"); s_res = sem("s_res")
        s_aw = sem("s_aw"); s_ac = sem("s_ac"); s_aw_ps = sem("s_aw_ps"); s_aw_c = sem("s_aw_c"); s_wa = sem("s_wa")
        s_xa = sem("s_xa"); s_xa_ps = sem("s_xa_ps"); s_xa_t = sem("s_xa_t"); s_qkvm_ps = sem("s_qkvm_ps")
        s_qkvm = sem("s_qkvm"); s_sq = sem("s_sq"); s_ss = sem("s_ss"); s_rs = sem("s_rs"); s_ms = sem("s_ms"); s_rr = sem("s_rr")
        s_kn = sem("s_kn"); s_q1 = sem("s_q1"); s_kpad = sem("s_kpad"); s_qpad = sem("s_qpad"); s_qf_ps = sem("s_qf_ps")
        s_qf = [sem(f"s_qf{i}") for i in range(2)]; s_res_a = sem("s_res_a"); s_v = sem("s_v"); s_z0 = sem("s_z0")
        s_kt_ps = sem("s_kt_ps"); s_qt_ps = sem("s_qt_ps"); s_kz = sem("s_kz"); s_qt = [sem(f"s_qt{i}") for i in range(2)]
        s_p1 = sem("s_p1"); s_max = sem("s_max"); s_nm = sem("s_nm"); s_p2 = sem("s_p2"); s_exp = sem("s_exp")
        s_pv = sem("s_pv"); s_ot = sem("s_ot"); s_or_ps = sem("s_or_ps"); s_or = sem("s_or"); s_den = sem("s_den")

        block = ctx.enter_context(nc.Block())
        UNITS = TG * (1 + NE)
        ALL, EARLY, LATE = slice(0, NT), slice(0, NT // 2), slice(NT // 2, NT)
        LN_MOE = (2, 5)

        def wait(eng, s, n):
            if not (isinstance(n, int) and n <= 0):
                eng.wait_ge(s, n)

        def within(b):
            return not isinstance(b, int) or b < B

        def pipelined(eng, step, start=0):
            if start == 0:
                step(0, 0, True, False)
            step(1, 1, False, False)
            with eng.Fori(1, B // 2 - 1) as i:
                step(2 * i, 0, False, False)
                step(2 * i + 1, 1, False, False)
            step(B - 2, 0, False, False)
            step(B - 1, 1, False, True)

        def end_phase(eng, n):
            eng.drain().then_inc(s_phase, 1)
            eng.wait_ge(s_phase, 4 * n)

        @block.sync
        def _(sp):
            def group_of(t, tg):
                return t.rearrange("(j p) d -> p j d", p=P)[:, GT * tg:GT * (tg + 1), :]

            for tg in range(TG):
                sp.dma_start(X[:, GT * tg:GT * (tg + 1), :], group_of(x, tg)).then_inc(s_x[tg], 16)
            sp.dma_start(w_in_s[:, :], w_in).then_inc(s_w_in, 16)
            for dst, src in ((conv_w_s[:, :, :], conv_w), (conv_b_s[:, :], conv_b)):
                sp.dma_start(dst, src).then_inc(s_w_conv, 16)
            for dst, src in ((idt_w[:, :, P:XRW], dt_w), (b_w_s[:, :, :], b_w), (c_w_s[:, :, :], c_w),
                             (w_out_s[:, :, :], w_out.rearrange("k p d -> p k d"))):
                sp.dma_start(dst, src).then_inc(s_w, 16)
            for i, src in enumerate((a_log, dt_b, d_skip)):
                sp.dma_start(row_nh[:, i, :], src.broadcast_to((P, NH))).then_inc(s_w, 16)
            for i, src in enumerate((ln_w, ln_b)):
                sp.dma_start(row_ln[:, i, :], src.broadcast_to((P, DI))).then_inc(s_w, 16)
            for dst, src in ((gate_w_s, gate_w), (w_dq_s, w_dq), (w_uq_s, w_uq_t), (w_dkv_s, w_dkv),
                             (w_ukv_s, w_ukv_t), (w_qr_s, w_qr), (w_kr_s, w_kr), (w_o_s, w_o_t)):
                sp.dma_start(dst[:, :], src).then_inc(s_aw, 16)
            for i, src in enumerate((qn_w, kn_w)):
                sp.dma_start(row_qk[:, i, :], src.broadcast_to((P, HD))).then_inc(s_aw, 16)

            def weights(m, k):
                if not (m == 0 and isinstance(k, int) and k == 0):
                    sp.wait_ge(s_split, 2 * ((1 + NE) * m + k))
                sp.dma_start(raw[:, 0, :], moe_w1[ds(k, 1), :, :].rearrange("e p n -> p (e n)")).then_inc(s_raw, 16)
                sp.dma_start(raw[:, 1, :], moe_w2[ds(k, 1), :, :, :].rearrange("e p c n -> p (e c n)")).then_inc(s_raw, 16)

            def gates_of(m, k, o):
                if not (isinstance(k, int) and k <= 2):
                    sp.wait_ge(s_gated, UNITS * m + TG * (k - 1))
                sp.dma_start(gates_b[:, o, :], gates_d[ds(NT * (k - 1), NT), :]
                             .rearrange("(o j) p -> o (j p)", o=1).broadcast_to((P, NT * P))).then_inc(s_gb[o], 16)

            for m in range(2):
                weights(m, 0)
                weights(m, 1)
                sp.wait_ge(s_gates_t, m + 1)
                sp.dma_start(gates_d, gates_t[:, :]).then_inc(s_gates_d, 16)
                sp.wait_ge(s_gates_d, 16 * (m + 1))
                for k in range(1, 3):
                    gates_of(m, k, k - 1)
                    weights(m, k + 1)
                with sp.Fori(1, NE // 2 - 1) as i:
                    for o in range(2):
                        gates_of(m, 2 * i + 1 + o, o)
                        weights(m, 2 * i + 2 + o)
                gates_of(m, NE - 1, 0)
                weights(m, NE)
                gates_of(m, NE, 1)
            for tg in range(TG):
                sp.wait_ge(s_res, TG + tg + 1)
                sp.dma_start(group_of(out, tg), X[:, GT * tg:GT * (tg + 1), :]).then_inc(s_out, 16)
            sp.wait_ge(s_out, 16 * TG)

        W_ALL = 16 * 9

        @block.gpsimd
        def _(pool):
            def split(m, k, o):
                pool.wait_ge(s_raw, 32 * ((1 + NE) * m + k + 1))
                if not (isinstance(k, int) and k < 2):
                    pool.wait_ge(s_down, UNITS * m + TG * (k - 1))
                pool.tensor_tensor(w_hi[:, o, :, :], raw[:, :, :], ident[:, P:P + 1].unsqueeze(2).broadcast_to((P, 2, HID)),
                                   ALU.add).then_inc(s_split, 1)
                pool.wait_ge(s_split, 2 * ((1 + NE) * m + k) + 1)
                pool.tensor_tensor(w_lo[:, o, :, :], raw[:, :, :], w_hi[:, o, :, :].bitcast(F32),
                                   ALU.subtract).then_inc(s_split, 1)

            def split_ahead(m, b):
                if isinstance(b, int) and b in (1, B - 2):
                    split(m, int(b > 1), int(b > 1))

            def moe_pool(m, phase):
                def add(n, tg, start=False):
                    pool.wait_ge(s_gated, n + 1)
                    part = acc[:, tg * GN:(tg + 1) * GN]
                    if start:
                        zero = ident[:, P:P + 1].broadcast_to((P, GN))
                        pool.tensor_tensor(part, gy[:, tg % 2, :], zero, ALU.add).then_inc(s_acc, 1)
                        return
                    pool.wait_ge(s_acc, n - TG + 1)
                    pool.tensor_tensor(part, part, gy[:, tg % 2, :], ALU.add).then_inc(s_acc, 1)

                for tg in range(TG):
                    add(UNITS * m + tg, tg, start=True)
                with pool.Fori(0, NE // 2 - 1) as i:
                    for o in range(2):
                        for tg in range(TG):
                            add(UNITS * m + TG * (2 * i + 1 + o) + tg, tg)
                            if tg == 0:
                                split(m, 2 * i + 2 + o, o)
                for o in range(2):
                    for tg in range(TG - o):
                        add(UNITS * m + TG * (NE - 1 + o) + tg, tg)
                        if tg == 0 and o == 0:
                            split(m, NE, 0)
                end_phase(pool, phase)

            def attn_pool():
                pool.memset(k_z[:, :, :, :, :].bitcast(F32), 0.0).then_inc(s_z0, 1)
                for pad in (q_pad, k_pad, v_pad):
                    pool.memset(pad[:, :, :, :, :], 0.0).then_inc(s_z0, 1)
                pool.wait_ge(s_z0, 4)
                pool.memset(k_pad[:, :, :, :, 3 * HD:3 * HD + 2], 1.0).then_inc(s_z0, 1)
                pool.memset(v_pad[:, :, :, :, HD:HD + 1], 1.0).then_inc(s_z0, 1)

                def prepare(b, o, first, last):
                    def section(i):
                        return QKVM[:, ds(TB * b, TB), i * D:(i + 1) * D].rearrange("p c (h e) -> p c h e", h=H)

                    def inverse(i):
                        return rr[:, ds(TB * b, TB), i * H:(i + 1) * H].unsqueeze(3).broadcast_to((P, TB, H, HD))

                    def heads(t):
                        return t.rearrange("p c (h e) -> p c h e", h=H)

                    def slots(pad, a):
                        return pad[:, o, :, :, a * HD:(a + 1) * HD].rearrange("p c h e -> p (c h) e")

                    def flat(t):
                        return t.rearrange("p c (h e) -> p (c h) e", h=H)

                    zero = ident[:, P:P + 1].unsqueeze(2)
                    wait(pool, s_kpad, 2 * b)
                    pool.tensor_tensor(heads(kn[:, 0, :, :]), section(1), inverse(1), ALU.mult).then_inc(s_kn, 1)
                    pool.wait_ge(s_kn, 3 * b + 1)
                    pool.tensor_tensor(kn[:, 1, :, :].rearrange("p c (h e) -> p (c h) e", h=H),
                                       kn[:, 0, :, :].rearrange("p c (h e) -> p (c h) e", h=H),
                                       row_qk[:, 2:3, :].broadcast_to((P, TB * H, HD)), ALU.mult).then_inc(s_kn, 1)
                    pool.wait_ge(s_kn, 3 * b + 2)
                    pool.tensor_tensor(heads(kn[:, 2, :, :]), heads(kn[:, 1, :, :]), section(3), ALU.add).then_inc(s_kn, 1)
                    if not first:
                        wait(pool, s_kt_ps, b - 1)
                    pool.wait_ge(s_kn, 3 * b + 3)
                    twice = k_pad[:, o, :, :, 0:2 * HD].rearrange("p c h (a e) -> p (c h) a e", a=2)
                    pool.tensor_tensor(twice.bitcast(F32R), flat(kn[:, 2, :, :]).unsqueeze(2).broadcast_to((P, TB * H, 2, HD)),
                                       zero.unsqueeze(3).broadcast_to((P, TB * H, 2, HD)), ALU.add).then_inc(s_kpad, 1)
                    pool.wait_ge(s_kpad, 2 * b + 1)
                    pool.tensor_tensor(slots(k_pad, 2).bitcast(F32R), flat(kn[:, 2, :, :]), slots(k_pad, 0),
                                       ALU.subtract).then_inc(s_kpad, 1)
                    wait(pool, s_qpad, 2 * b)
                    pool.tensor_tensor(heads(q1[:, :, :]), section(0), inverse(0), ALU.mult).then_inc(s_q1, 1)
                    if not first:
                        wait(pool, s_qf_ps, 2 * (b - 1))
                    pool.wait_ge(s_q1, 2 * b + 1)
                    ends = q_pad[:, o, :, :, 0:3 * HD].rearrange("p c h (a e) -> p (c h) a e", a=3)[:, :, 0:3:2, :]
                    pool.tensor_tensor(ends.bitcast(F32R), flat(q1[:, :, :]).unsqueeze(2).broadcast_to((P, TB * H, 2, HD)),
                                       zero.unsqueeze(3).broadcast_to((P, TB * H, 2, HD)), ALU.add).then_inc(s_qpad, 1)
                    pool.memset(q_pad[:, o, :, :, 3 * HD:3 * HD + 2], 0.0).then_inc(s_q1, 1)
                    pool.wait_ge(s_qpad, 2 * b + 1)
                    pool.tensor_tensor(slots(q_pad, 1).bitcast(F32R), flat(q1[:, :, :]), slots(q_pad, 0),
                                       ALU.subtract).then_inc(s_qpad, 1)
                    if not first:
                        wait(pool, s_pv, NG * (b - 1))
                    pool.tensor_tensor(v_pad[:, o, :, :, 0:HD], section(2), zero.unsqueeze(3).broadcast_to((P, TB, H, HD)),
                                       ALU.add).then_inc(s_v, 1)
                    split_ahead(1, b)

                pool.wait_ge(s_qkvm, TB)
                pool.wait_ge(s_rr, 1)
                prepare(0, 0, True, False)
                pool.wait_ge(s_qkvm, TB * B)
                pool.wait_ge(s_rr, 2)
                pipelined(pool, prepare, 1)

            pool.memset(ident[:, :], 0.0).then_inc(s_const, 1)
            pool.memset(x_pad[:, :, :, 0:TAPS - 1], 0.0).then_inc(s_const, 1)
            pool.memset(c_z[:, :, :], 0.0).then_inc(s_const, 1)
            pool.wait_ge(s_const, 3)
            pool.affine_select(out=ident[:, 0:P], in_=ident[:, 0:P], compare_op=ALU.not_equal, fill=1.0,
                               base=0, pattern=[[-1, P]], channel_multiplier=1).then_inc(s_const, 1)
            pool.wait_ge(s_const, 4)
            pool.iota(iota_i[:, :], pattern=[[1, NE]], base=0, channel_multiplier=0).then_inc(s_ac, 1)
            pool.memset(mask_ts[:, :, :], 0.0).then_inc(s_ac, 1)
            pool.memset(mask_st[:, :, :], 0.0).then_inc(s_ac, 1)
            pool.memset(head_of[:, :], 1.0).then_inc(s_ac, 1)
            pool.wait_ge(s_ac, 4)
            pool.tensor_copy(iota[:, :], iota_i[:, :]).then_inc(s_ac, 1)
            pool.affine_select(out=mask_ts[:, :, :], in_=mask_ts[:, :, :], compare_op=ALU.is_ge, fill=MASKED,
                               base=0, pattern=[[0, 2], [-1, P]], channel_multiplier=1).then_inc(s_ac, 1)
            pool.affine_select(out=mask_st[:, :, :], in_=mask_st[:, :, :], compare_op=ALU.is_ge, fill=MASKED,
                               base=0, pattern=[[0, 2], [1, P]], channel_multiplier=-1).then_inc(s_ac, 1)
            pool.affine_select(out=head_of[:, :], in_=head_of[:, :], compare_op=ALU.is_ge, fill=0.0,
                               base=0, pattern=[[-HD, H]], channel_multiplier=1).then_inc(s_ac, 1)
            pool.wait_ge(s_ac, 8)
            pool.affine_select(out=head_of[:, :], in_=head_of[:, :], compare_op=ALU.is_ge, fill=0.0,
                               base=HD - 1, pattern=[[HD, H]], channel_multiplier=-1).then_inc(s_ac, 1)
            pool.tensor_copy(ident_b[:, :], ident[:, 0:P]).then_inc(s_ac, 1)
            pool.tensor_copy(rep8[:, :, :], ident[0:HD, 0:HD].unsqueeze(1).broadcast_to((HD, H, HD))).then_inc(s_ac, 1)
            pool.wait_ge(s_w, W_ALL)
            for k in range(KI):
                pool.tensor_copy(idt_w[:, k, 0:P], ident[:, 0:P]).then_inc(s_const, 1)
            def z_parts(b, o, first, last):
                pool.wait_ge(s_z, b + 1)
                for i, dst in enumerate((ZW, ZB)):
                    pool.tensor_tensor(dst[:, ds(TB * b, TB), :], z_act[:, o, :, :],
                                       row_ln[:, i:i + 1, :].broadcast_to((P, TB, DI)), ALU.mult).then_inc(s_zw, 1)

            pipelined(pool, z_parts)
            pool.wait_ge(s_dtv, 11)
            pool.wait_ge(s_xr, TB * B)

            def inputs_of(b, o):
                if not (isinstance(b, int) and b < 2):
                    pool.wait_ge(s_y, TB * (b - 1))
                for c in range(TB):
                    rows = XR[:, ds(TB * b + c, 1), :, 0:P].rearrange("p o k (h e) -> p (o k) h e", h=NH // KI)
                    pool.tensor_tensor(
                        xdt[:, o, c, :].rearrange("p (k h e) -> p k h e", k=KI, h=NH // KI), rows,
                        DT[:, ds(TB * b + c, 1), :].rearrange("p o (k h) -> p (o k) h", k=KI).unsqueeze(3)
                        .broadcast_to((P, KI, NH // KI, HP)), ALU.mult).then_inc(s_xdt, 1)
                    pool.tensor_tensor(
                        dx[:, o, c, :].rearrange("p (k h e) -> p k h e", k=KI, h=NH // KI), rows,
                        row_nh[:, 2, :].rearrange("p (k h) -> p k h", k=KI).unsqueeze(3)
                        .broadcast_to((P, KI, NH // KI, HP)), ALU.mult).then_inc(s_xdt, 1)

            def scan_step(b, o, first, last):
                if not last:
                    inputs_of(b + 1, 1 - o)
                pool.wait_ge(s_yn, b + 1)
                pool.tensor_tensor(yw[:, :, :], yn[:, :, :], ZW[:, ds(TB * b, TB), :], ALU.mult).then_inc(s_yw, 1)
                pool.wait_ge(s_yw, b + 1)
                wait(pool, s_gt_ps, b)
                pool.tensor_tensor(g[:, :, :], yw[:, :, :], ZB[:, ds(TB * b, TB), :], ALU.add).then_inc(s_g, 1)
                split_ahead(0, b)

            inputs_of(0, 0)
            pipelined(pool, scan_step)
            end_phase(pool, 1)
            moe_pool(0, 2)
            attn_pool()
            end_phase(pool, 3)
            moe_pool(1, 4)

        @block.scalar
        def _(act):
            def ln_root(n, tiles):
                act.wait_ge(s_lnv, n)
                act.activation(std[:, tiles], var[:, tiles], ACT.Sqrt).then_inc(s_std, 1)

            def rows_turned(m, tg):
                n = TG * m + tg
                act.wait_ge(s_xt_ps, n + 1)
                wait(act, s_lg_ps, n - 1)
                wait(act, s_xl, 2 * (n - 1))
                act.copy(xt4[:, tg % 2, :], PS[:, 6 - tg % 2, :]).then_inc(s_xt, 1)

            ln_root(1, ALL)

            def front(b, o):
                act.wait_ge(s_xn_ps, b + 1)
                act.copy(xn_t[:, o, :], PS[:, 5 * o, 0:T]).then_inc(s_xn_t, 1)

            def split_up(b, o):
                act.wait_ge(s_xc_ps, b + 1)
                wait(act, s_tap, KI * (TAPS - 1) * (b - 1))
                xc = PS[:, 1 + 5 * o, :].rearrange("p (k t) -> p k t", k=KI)
                act.copy(x_pad[:, o, :, TAPS - 1:], xc).then_inc(s_xpad, 1)
                wait(act, s_xs_t, KI * (b - 1))
                for k in range(KI):
                    act.mul(conv_o[:, o, k, :], xc[:, k, :], conv_w_s[:, k, TAPS - 1:TAPS]).then_inc(s_tap0, 1)
                if within(b + 1):
                    front(b + 1, 1 - o)
                act.wait_ge(s_z_ps, b + 1)
                wait(act, s_zw, 2 * (b - 1))
                act.activation(z_act[:, o, :, :], PS[:, 2 + 5 * o, :].rearrange("p (c n) -> p c n", c=TB), ACT.Silu).then_inc(s_z, 1)

            def rows_copy(b):
                act.wait_ge(s_xr_ps, b + 1)
                for c in range(TB):
                    act.copy(XR[:, ds(TB * b + c, 1), :, :].rearrange("p o k n -> p (o k) n"),
                             PS[:, 3 + c, 0:KI * XRW].rearrange("p (k n) -> p k n", k=KI)).then_inc(s_xr, 1)

            def front_step(b, o, first, last):
                if not (isinstance(b, int) and b < 2):
                    rows_copy(b - 2)
                if not last:
                    split_up(b + 1, 1 - o)
                act.wait_ge(s_tap, KI * (TAPS - 1) * (b + 1))
                wait(act, s_xst, b - 1)
                for k in range(KI):
                    act.activation(xs_t[:, o, k, :], conv_o[:, o, k, :], ACT.Silu, bias=conv_b_s[:, k:k + 1]).then_inc(s_xs_t, 1)

            front(0, 0)
            act.wait_ge(s_w_conv, 32)
            split_up(0, 0)
            pipelined(act, front_step)
            rows_copy(B - 2)
            rows_copy(B - 1)
            def bc_copy(b):
                act.wait_ge(s_bc_ps, b + 1)
                act.copy(b_t[:, :, :], PS[:, 0, :].rearrange("p (q t) -> p q t", q=KI)).then_inc(s_bc, 1)
                for r in range(2):
                    half = slice(HP * r, HP * (r + 1))
                    act.copy(c_z[half, r:NH:2, :], PS[half, 1, :].rearrange("p (q t) -> p q t", q=KI)).then_inc(s_bc, 1)

            act.wait_ge(s_w, W_ALL)
            act.activation(neg_a[:, :], row_nh[:, 0, :], ACT.Exp).then_inc(s_dta, 1)
            act.wait_ge(s_dtv, 3)
            act.activation(tmp[2][:, :, :], tmp[1][:, :, :], ACT.Exp).then_inc(s_dta, 1)
            act.wait_ge(s_dtv, 4)
            act.activation(tmp[4][:, :, :], tmp[3][:, :, :], ACT.Ln).then_inc(s_dta, 1)
            act.wait_ge(s_const, 3)
            bc_copy(0)
            act.wait_ge(s_dtv, 12)
            act.activation(AB[:, :, :], tmp[1][:, :, :], ACT.Exp, scale=-1.0).then_inc(s_dta, 1)

            def gate_copy(b):
                act.wait_ge(s_gt_ps, b + 1)
                act.copy(g_t[:, :, :], PS[:, 0, :].rearrange("p (k t) -> p k t", k=KI)).then_inc(s_gt, 1)

            def y_std(b):
                act.wait_ge(s_ymv, TB * (b + 1))
                act.activation(ysd[:, :], ymv[:, :, 1], ACT.Sqrt, bias=LN_EPS).then_inc(s_ysd, 1)

            def ab_copy(b, o):
                if not (isinstance(b, int) and b < 2):
                    act.wait_ge(s_g_ps, KI * (b - 1))
                act.copy(ab_b[:, o, :, :], AB[:, ds(TB * b, TB), :]).then_inc(s_ab, 1)

            def scan_step(b, o, first, last):
                if not last:
                    ab_copy(b + 1, 1 - o)
                    bc_copy(b + 1)
                if not first:
                    gate_copy(b - 1)
                if last:
                    ln_root(LN_MOE[0], EARLY)
                y_std(b)

            act.wait_ge(s_dta, 4)
            ab_copy(0, 0)
            pipelined(act, scan_step)
            rows_turned(0, 0)
            gate_copy(B - 1)
            rows_turned(0, 1)
            end_phase(act, 1)

            def moe_act(m, phase):
                ln_root(LN_MOE[m] + 1, LATE)

                def hidden(n, tg):
                    o = tg % 2
                    for h in range(2):
                        act.wait_ge(s_up, 2 * n + h + 1)
                        if not (isinstance(n, int) and n < 2):
                            act.wait_ge(s_lo, 2 * (n - 1))
                        act.activation(h_f[:, o, h, :], PS[:, 2 * h:2 * h + 2, :].rearrange("p c t -> p (c t)"),
                                       ACT.Silu).then_inc(s_silu, 1)

                def high(n, tg):
                    if not (isinstance(n, int) and n < 2):
                        act.wait_ge(s_down, n - 1)
                    for h in range(2):
                        act.wait_ge(s_silu, 2 * n + h + 1)
                        act.copy(h_hi[:, tg % 2, h, :], h_f[:, tg % 2, h, :]).then_inc(s_hi, 1)

                def unit(n, tg):
                    hidden(n, tg)
                    high(n, tg)

                hidden(UNITS * m, 0)
                rows_turned(m, 2)
                high(UNITS * m, 0)
                rows_turned(m, 3)
                unit(UNITS * m + 1, 1)
                act.wait_ge(s_top, m + 1)
                act.activation(top_g[:, 1, :], top_g[:, 0, :], ACT.Exp).then_inc(s_e, 1)
                for tg in range(2, TG):
                    unit(UNITS * m + tg, tg)
                with act.Fori(0, NE) as e:
                    for tg in range(TG):
                        unit(UNITS * m + TG * (e + 1) + tg, tg)
                end_phase(act, phase)

            def attn_act():
                ln_root(4, ALL)

                def columns(b, o):
                    act.wait_ge(s_xa_ps, b + 1)
                    act.copy(xa_t[:, o, :], PS[:, 5 * o, 0:T]).then_inc(s_xa_t, 1)

                def front_step(b, o, first, last):
                    if not last:
                        columns(b + 1, 1 - o)
                    for c in range(TB):
                        act.wait_ge(s_qkvm_ps, TB * b + c + 1)
                        if c == 0:
                            wait(act, s_ss, TB * (b - 1))
                        act.activation(sq[:, o, c, :], PS[:, 1 + 5 * o + c, 0:2 * D], ACT.Square).then_inc(s_sq, 1)
                        act.copy(QKVM[:, ds(TB * b + c, 1), :].rearrange("p o n -> p (o n)"),
                                 PS[:, 1 + 5 * o + c, :]).then_inc(s_qkvm, 1)
                    if isinstance(b, int) and b == 1:
                        roots(0)

                def roots(part):
                    tiles = (slice(0, TB), slice(TB, NT))[part]
                    act.wait_ge(s_ms, part + 1)
                    act.activation(rr[:, tiles, :], ss[:, tiles, :], ACT.Sqrt).then_inc(s_rs, 1)

                columns(0, 0)
                pipelined(act, front_step)
                roots(1)
                act.wait_ge(s_z0, 6)

                def banks(a):
                    return PS[:, a:a + 2, :].rearrange("p k (g t) -> p (k g) t", g=2)

                def keys(b, o, j0=0, j1=4):
                    act.wait_ge(s_kt_ps, b + 1)
                    for j in range(j0, j1):
                        lanes = slice(SLOT * j, SLOT * (j + 1))
                        act.copy(k_z[lanes, o, :, j, :], banks(0)[lanes, :, :]).then_inc(s_kz, 1)

                def queries(b):
                    act.wait_ge(s_qt_ps, b + 1)
                    act.copy(q_t[:, 0, 0:2, :], PS[:, 2, :].rearrange("p (g t) -> p g t", g=2)).then_inc(s_qt[0], 1)

                def outputs(b):
                    act.wait_ge(s_pv, NG * (b + 1))
                    wait(act, s_or_ps, b)
                    act.copy(o_t[:, :, :], banks(0)).then_inc(s_ot, 1)

                def step(b, o, first, last):
                    if not first:
                        outputs(b - 1)
                    if not last:
                        keys(b + 1, 1 - o, 0, 3)
                    act.wait_ge(s_qf_ps, 2 * b + 1)
                    act.copy(q_t[:, 1, 0:2, :], PS[:, 2, :].rearrange("p (g t) -> p g t", g=2)).then_inc(s_qf[0], 1)
                    if not last:
                        keys(b + 1, 1 - o, 3, 4)
                    for g_ in range(NG):
                        for c in range(TB):
                            i = TB * g_ + c
                            act.wait_ge(s_p2, 8 * b + i + 1)
                            wait(act, s_pv, NG * b + g_ - 1)
                            src = banks(4 + 2 * (i % 2))
                            dst = probs[:, g_ % 2, :, :]
                            act.activation(dst[:, :, T:T + P] if c else dst[:, :, 0:T], src[:, :, P:T] if c else src,
                                           ACT.Exp).then_inc(s_exp, 1)
                            if i == 5 and not last:
                                queries(b + 1)

                keys(0, 0)
                queries(0)
                pipelined(act, step)
                ln_root(LN_MOE[1], EARLY)
                outputs(B - 1)
                rows_turned(1, 0)
                rows_turned(1, 1)
                end_phase(act, 3)

            moe_act(0, 2)
            attn_act()
            moe_act(1, 4)

        @block.tensor
        def _(pe):
            def front(b, o):
                pe.wait_ge(s_xn, TB * (b + 1))
                wait(pe, s_xn_t, b - 1)
                for c in range(TB):
                    m = pe.transpose(PS[:, 5 * o, c * P:(c + 1) * P], xn[:, o, c, :], ident[:, 0:P])
                m.then_inc(s_xn_ps, 1)

            def project_in(b, o):
                pe.wait_ge(s_xn_t, b + 1)
                wait(pe, s_tap0, KI * (b - 1))
                for k in range(KI):
                    m = pe.matmul(PS[:, 1 + 5 * o, k * T:(k + 1) * T], w_in_s[:, k * P:(k + 1) * P], xn_t[:, o, :],
                                  start=True, stop=True)
                m.then_inc(s_xc_ps, 1)
                wait(pe, s_z, b - 1)
                for c in range(TB):
                    m = pe.matmul(PS[:, 2 + 5 * o, c * DI:(c + 1) * DI], xn_t[:, o, c * P:(c + 1) * P], w_in_s[:, DI:2 * DI],
                                  start=True, stop=True)
                m.then_inc(s_z_ps, 1)

            def front_step(b, o, first, last):
                if not last:
                    project_in(b + 1, 1 - o)
                if within(b + 2):
                    front(b + 2, o)
                if not first:
                    rows(b - 1, 1 - o)

            def rows(b, o):
                if isinstance(b, int) and b == 0:
                    pe.wait_ge(s_const, 4 + KI)
                    pe.wait_ge(s_w, W_ALL)
                pe.wait_ge(s_xs_t, KI * (b + 1))
                wait(pe, s_xr, TB * b)
                for c in range(TB):
                    for k in range(KI):
                        m = pe.matmul(PS[:, 3 + c, k * XRW:(k + 1) * XRW], xs_t[:, o, k, c * P:(c + 1) * P],
                                      idt_w[:, k, :], start=True, stop=True)
                m.then_inc(s_xr_ps, 1)

            pe.wait_ge(s_const, 4)
            pe.wait_ge(s_w_in, 16)
            front(0, 0)
            front(1, 1)
            project_in(0, 0)
            pipelined(pe, front_step)
            rows(B - 1, 1)

            def bc(b):
                for bank, w in ((0, b_w_s), (1, c_w_s)):
                    for q in range(KI):
                        for k in range(KI):
                            m = pe.matmul(PS[:, bank, q * T:(q + 1) * T], w[:, k, q * P:(q + 1) * P],
                                          XST[:, k, ds(b * T, T)], start=k == 0, stop=k == KI - 1)
                m.then_inc(s_bc_ps, 1)

            def scores(b, o, q):
                pe.wait_ge(s_bc, 3 * (b + 1))
                wait(pe, s_y, TB * b)
                for r in range(2):
                    pe.matmul(PS[:, 2 + 3 * q, r * T:(r + 1) * T], b_t[:, q, 0:P], c_z[:, 2 * q + r, :],
                              start=True, stop=True)
                for r in range(2):
                    pe.matmul(PS[:, 3 + 3 * q, r * P:(r + 1) * P], b_t[:, q, P:T], c_z[:, 2 * q + r, P:T],
                              start=True, stop=True)
                pe.wait_ge(s_ab, b + 1)
                for r in range(2):
                    for c in range(TB):
                        h = 2 * q + r
                        m = pe.transpose(PS[:, 4 + 3 * q, r * T + c * P:r * T + (c + 1) * P],
                                         ab_b[:, o, c, h:h + 1].broadcast_to((P, P)), ident[:, 0:P])
                m.then_inc(s_g_ps, 1)

            def y_rows(b, o):
                pe.wait_ge(s_wq, 2 * KI * (b + 1))
                pe.wait_ge(s_xdt, 2 * TB * (b + 1))
                for c in range(TB):
                    for h in range(NH):
                        q, r = h // 2, h % 2
                        y_ = PS[:, 2 + 3 * c, h * P:(h + 1) * P]
                        if c == 0:
                            m = pe.matmul(y_, w0[:, q, r, 0:P], xdt[:, o, 0, q * P:(q + 1) * P], start=True, stop=True)
                        else:
                            pe.matmul(y_, w0[:, q, r, P:T], xdt[:, o, 0, q * P:(q + 1) * P], start=True, stop=False)
                            m = pe.matmul(y_, w1[:, q, r, :], xdt[:, o, 1, q * P:(q + 1) * P], start=False, stop=True)
                    m.then_inc(s_y_ps, 1)

            def turn(b, copied):
                pe.wait_ge(s_g, b + 1)
                pe.wait_ge(s_bc, 3 * (copied + 1))
                for k in range(KI):
                    for c in range(TB):
                        m = pe.transpose(PS[:, 0, k * T + c * P:k * T + (c + 1) * P], g[:, c, k * P:(k + 1) * P],
                                         ident[:, 0:P])
                m.then_inc(s_gt_ps, 1)

            def project(b):
                pe.wait_ge(s_gt, b + 1)
                for c in range(TB):
                    for k in range(KI):
                        m = pe.matmul(PS[:, 1, c * P:(c + 1) * P], g_t[:, k, c * P:(c + 1) * P], w_out_s[:, k, :],
                                      start=k == 0, stop=k == KI - 1)
                m.then_inc(s_o_ps, 1)

            def group_columns(m, tg):
                pe.wait_ge(s_xn4, TG * m + tg + 1)
                wait(pe, s_xt, TG * m + tg - 1)
                for i in range(GT):
                    mm = pe.transpose(PS[:, 6 - tg % 2, i * P:(i + 1) * P], xn4[:, tg % 2, i, :], ident[:, 0:P])
                mm.then_inc(s_xt_ps, 1)

            def scan_step(b, o, first, last):
                early = isinstance(b, int) and b < 2
                scores(b, o, 0)
                if not early:
                    project(b - 2)
                scores(b, o, 1)
                if not last:
                    if not early:
                        pe.wait_ge(s_o, b - 1)
                    bc(b + 1)
                y_rows(b, o)
                if not first:
                    turn(b - 1, b if last else b + 1)

            pe.wait_ge(s_xst, B)
            pe.wait_ge(s_xn_t, B)
            pe.wait_ge(s_tap0, KI * B)
            bc(0)
            pe.wait_ge(s_z, B)
            pe.wait_ge(s_xr, TB * B)
            pipelined(pe, scan_step)
            project(B - 2)
            pe.wait_ge(s_y, TB * B)
            group_columns(0, 0)
            turn(B - 1, B - 1)
            group_columns(0, 1)
            pe.wait_ge(s_o, B - 1)
            project(B - 1)
            end_phase(pe, 1)

            def moe_pe(m, phase):
                pe.wait_ge(s_aw, 16 * 10)
                def logits_of(tg):
                    n = TG * m + tg
                    pe.wait_ge(s_xt, n + 1)
                    wait(pe, s_lg, n - 1)
                    for i in range(GT):
                        mm = pe.matmul(PS[:, 7 - 3 * (tg % 2), i * NE:(i + 1) * NE], xt4[:, tg % 2, i * P:(i + 1) * P],
                                       gate_w_s[:, :], start=True, stop=True)
                    mm.then_inc(s_lg_ps, 1)

                def up(k, tg, o):
                    n = UNITS * m + TG * k + tg
                    if isinstance(k, int) and k == 0:
                        pe.wait_ge(s_xl, 2 * (TG * m + tg + 1))
                    if tg == 0:
                        pe.wait_ge(s_split, 2 * ((1 + NE) * m + k + 1))
                    cols = slice(tg * GN, (tg + 1) * GN)
                    for h in range(2):
                        if not (isinstance(n, int) and n == 0):
                            pe.wait_ge(s_silu, 2 * n + h - 1)
                        for c in (2 * h, 2 * h + 1):
                            hi, lo = (w[:, o, 0, c * P:(c + 1) * P] for w in (w_hi, w_lo))
                            pe.matmul(PS[:, c, :], hi, XH[:, cols], start=True, stop=False)
                            pe.matmul(PS[:, c, :], hi, XL[:, cols], start=False, stop=False)
                            mm = pe.matmul(PS[:, c, :], lo, XH[:, cols], start=False, stop=True)
                        mm.then_inc(s_up, 1)

                def down(k, tg, o):
                    n = UNITS * m + TG * k + tg
                    if not (isinstance(n, int) and n < 2):
                        pe.wait_ge(s_gated, n - 1)
                    bank = PS[:, 4 + tg % 2, :]
                    for h in range(2):
                        pe.wait_ge(s_lo, 2 * n + h + 1)
                        for i in range(2):
                            c = 2 * h + i
                            hi, lo = (w[:, o, 1, c * P:(c + 1) * P] for w in (w_hi, w_lo))
                            a_hi, a_lo = (a[:, tg % 2, h, i * GN:(i + 1) * GN] for a in (h_hi, h_lo))
                            pe.matmul(bank, hi, a_hi, start=c == 0, stop=False)
                            pe.matmul(bank, hi, a_lo, start=False, stop=False)
                            mm = pe.matmul(bank, lo, a_hi, start=False, stop=c == CH - 1)
                    mm.then_inc(s_down, 1)

                def back(tg):
                    pe.wait_ge(s_acc, UNITS * m + TG * NE + tg + 1)
                    if tg >= 2:
                        pe.wait_ge(s_res, TG * m + tg - 1)
                    for i in range(GT):
                        mm = pe.transpose(PS[:, 6 + tg % 2, i * P:(i + 1) * P], acc[:, tg * GN + i * P:tg * GN + (i + 1) * P],
                                          ident[:, 0:P])
                    mm.then_inc(s_acc_ps, 1)

                def expert(k, o, first=False, last=False):
                    for tg in range(TG):
                        if tg < TG - 1:
                            if not (first and tg == 0):
                                up(k, tg + 1, o)
                        elif not last:
                            up(k + 1, 0, 1 - o)
                        down(k, tg, o)
                        if first and tg == 1:
                            pe.wait_ge(s_gates, m + 1)
                            pe.transpose(PS[:, 7, 0:P], gates[:, :, :].rearrange("p e j -> p (e j)"),
                                         ident[:, 0:P]).then_inc(s_gates_ps, 1)
                        if last and tg == 2:
                            back(0)
                            back(1)

                logits_of(0)
                logits_of(1)
                up(0, 0, 0)
                group_columns(m, 2)
                group_columns(m, 3)
                logits_of(2)
                up(0, 1, 0)
                logits_of(3)
                pe.wait_ge(s_lg, TG * (m + 1))
                expert(0, 0, first=True)
                with pe.Fori(0, NE // 2 - 1) as i:
                    expert(2 * i + 1, 1)
                    expert(2 * i + 2, 0)
                expert(NE - 1, 1)
                expert(NE, 0, last=True)
                for tg in range(2, TG):
                    back(tg)
                end_phase(pe, phase)

            def attn_pe():
                pe.wait_ge(s_ac, 11)
                pe.wait_ge(s_aw, 16 * 10)
                pe.matmul(PS[0:HD, 7, 0:HD], w_dq_s[:, :], w_uq_s[:, :], start=True, stop=True)
                pe.matmul(PS[0:HD, 7, HD:2 * HD], w_dkv_s[:, :], w_ukv_s[:, 0:HD], start=True, stop=True)
                pe.matmul(PS[0:HD, 7, 3 * HD:4 * HD], w_kr_s[:, :], w_qr_s[:, :], start=True, stop=True)
                pe.matmul(PS[0:HD, 7, 4 * HD:5 * HD], w_ukv_s[:, HD:2 * HD], w_dkv_s[:, :], start=True, stop=True).then_inc(s_aw_ps, 1)
                pe.wait_ge(s_aw_c, 3)
                pe.matmul(PS[0:HD, 6, 0:HD], av[:, :], w_o_s[:, :], start=True, stop=True).then_inc(s_aw_ps, 1)
                pe.wait_ge(s_aw_c, 4)
                pe.matmul(PS[:, 7, 0:NSEC * HD], rep8[:, :, :].rearrange("e h f -> e (h f)"), small[:, :],
                          start=True, stop=True).then_inc(s_aw_ps, 1)

                def columns(b, o):
                    pe.wait_ge(s_xa, TB * (b + 1))
                    wait(pe, s_xa_t, b - 1)
                    for c in range(TB):
                        mm = pe.transpose(PS[:, 5 * o, c * P:(c + 1) * P], xa[:, o, c, :], ident[:, 0:P])
                    mm.then_inc(s_xa_ps, 1)

                def front_step(b, o, first, last):
                    if not last:
                        columns(b + 1, 1 - o)
                    pe.wait_ge(s_xa_t, b + 1)
                    if not first:
                        wait(pe, s_qkvm, TB * (b - 1))
                    for c in range(TB):
                        pe.matmul(PS[:, 1 + 5 * o + c, :], xa_t[:, o, c * P:(c + 1) * P],
                                  w_all[:, :, :, :].rearrange("p s h e -> p (s h e)"), start=True, stop=True).then_inc(s_qkvm_ps, 1)

                columns(0, 0)
                pe.wait_ge(s_wa, NSEC + 1)
                pipelined(pe, front_step)

                def to_columns(pad, bank, groups):
                    for g_ in groups:
                        for c in range(TB):
                            mm = pe.transpose(PS[:, bank + g_ // 2, (g_ % 2) * T + c * P:(g_ % 2) * T + (c + 1) * P],
                                              pad[:, c, 4 * g_:4 * g_ + 4, :].rearrange("p h s -> p (h s)"), ident[:, 0:P])
                    return mm

                def keys(b, o):
                    pe.wait_ge(s_kpad, 2 * (b + 1))
                    wait(pe, s_ot, b - 1)
                    to_columns(k_pad[:, o], 0, range(NG)).then_inc(s_kt_ps, 1)

                def queries(b, o):
                    pe.wait_ge(s_qpad, 2 * (b + 1))
                    pe.wait_ge(s_q1, 2 * (b + 1))
                    wait(pe, s_qf[0], b)
                    wait(pe, s_qf[1], b)
                    wait(pe, s_or, b - 1)
                    to_columns(q_pad[:, o], 2, range(NG)).then_inc(s_qt_ps, 1)

                def queries_less_max(b, o, half):
                    pe.wait_ge(s_nm, 4 * b + 2 * (half + 1))
                    to_columns(q_pad[:, o], 2, range(2 * half, 2 * half + 2)).then_inc(s_qf_ps, 1)

                def mask_two(bank, c, mask):
                    return pe.matmul(PS[:, bank, :].rearrange("p (h t) -> p h t", h=2)[:, :, c * P:(c + 1) * P],
                                     ident_b[:, :], mask[:, :, :], start=False, stop=True)

                def maxima(b, o, g_):
                    for c in range(TB):
                        i = TB * g_ + c
                        if i < 2:
                            wait(pe, s_exp, 8 * b + i - 1)
                        else:
                            pe.wait_ge(s_max, 8 * b + i - 1)
                        for j in range(4):
                            bank, at = 4 + 2 * (i % 2) + j // 2, (j % 2) * T
                            pe.matmul(PS[:, bank, at:at + T], q_t[:, 0, g_, c * P:(c + 1) * P], k_z[:, o, g_, j, :],
                                      start=j % 2 == 0, stop=False)
                            if j % 2:
                                mm = mask_two(bank, c, mask_ts)
                        mm.then_inc(s_p1, 1)

                def scores_less_max(b, o, i):
                    g_, c = i // TB, i % TB
                    if i < 2:
                        pe.wait_ge(s_max, 8 * b + 7 + i)
                    else:
                        pe.wait_ge(s_exp, 8 * b + i - 1)
                    for j in range(4):
                        bank, at = 4 + 2 * (i % 2) + j // 2, (j % 2) * T
                        pe.matmul(PS[:, bank, at:at + T], k_z[:, o, g_, j, c * P:(c + 1) * P], q_t[:, 1, g_, :],
                                  start=j % 2 == 0, stop=False)
                        if j % 2:
                            mm = mask_two(bank, c, mask_st)
                    mm.then_inc(s_p2, 1)

                def values(b, o, i):
                    g_, c = i // TB, i % TB
                    pe.wait_ge(s_exp, 8 * b + i + 1)
                    for j in range(4):
                        at = (g_ % 2) * T + c * P
                        mm = pe.matmul(PS[SLOT * j:SLOT * (j + 1), g_ // 2, at:(g_ % 2 + 1) * T],
                                       v_pad[:, o, c, 4 * g_ + j, :],
                                       probs[:, g_ % 2, j, T:T + P] if c else probs[:, g_ % 2, j, 0:T],
                                       start=c == 0, stop=c == 1, skip_group_check=True)
                    if c == 1:
                        mm.then_inc(s_pv, 1)

                def last_values(b, o):
                    for i in range(6, 8):
                        values(b, o, i)

                def output_rows(b):
                    pe.wait_ge(s_ot, b + 1)
                    wait(pe, s_or, b)
                    for c in range(TB):
                        for g_ in range(NG):
                            mm = pe.transpose(PS[:, 2 + c, g_ * P:(g_ + 1) * P], o_t[:, g_, c * P:(c + 1) * P], ident[:, 0:P])
                    mm.then_inc(s_or_ps, 1)

                def step(b, o, first, last):
                    pe.wait_ge(s_kz, 4 * (b + 1))
                    pe.wait_ge(s_qt[0], b + 1)
                    maxima(b, o, 0)
                    if not first:
                        last_values(b - 1, 1 - o)
                    maxima(b, o, 1)
                    if not last:
                        keys(b + 1, 1 - o)
                    pe.wait_ge(s_qt[1], b + 1)
                    maxima(b, o, 2)
                    queries_less_max(b, o, 0)
                    maxima(b, o, 3)
                    pe.wait_ge(s_qf[0], b + 1)
                    scores_less_max(b, o, 0)
                    scores_less_max(b, o, 1)
                    queries_less_max(b, o, 1)
                    scores_less_max(b, o, 2)
                    pe.wait_ge(s_v, b + 1)
                    pe.wait_ge(s_kz, 4 * (b + 1 if last else b + 2))
                    values(b, o, 0)
                    scores_less_max(b, o, 3)
                    values(b, o, 1)
                    pe.wait_ge(s_qf[1], b + 1)
                    if not first:
                        output_rows(b - 1)
                    scores_less_max(b, o, 4)
                    values(b, o, 2)
                    scores_less_max(b, o, 5)
                    if not last:
                        queries(b + 1, 1 - o)
                    values(b, o, 3)
                    scores_less_max(b, o, 6)
                    scores_less_max(b, o, 7)
                    values(b, o, 4)
                    values(b, o, 5)

                pe.wait_ge(s_z0, 6)
                pe.wait_ge(s_xa_t, B)
                pe.wait_ge(s_qkvm, TB * B)
                keys(0, 0)
                queries(0, 0)
                pipelined(pe, step)
                last_values(B - 1, 1)
                group_columns(1, 0)
                output_rows(B - 1)
                group_columns(1, 1)
                end_phase(pe, 3)

            moe_pe(0, 2)
            attn_pe()
            moe_pe(1, 4)

        @block.vector
        def _(dve):
            def tile_stats(j0, n):
                for i in range(n):
                    dve.bn_stats(stats[:, ds(j0 + i, 1), :].rearrange("p o s -> p (o s)"),
                                 X[:, ds(j0 + i, 1), :].rearrange("p o s -> p (o s)"))

            def ln_variance(tiles):
                dve.drain()
                total, gap, squares, half = (mtmp[:, i, tiles] for i in range(4))
                dve.tensor_tensor(total, stats[:, tiles, 1], stats[:, tiles, 4], ALU.add)
                dve.tensor_tensor(gap, stats[:, tiles, 1], stats[:, tiles, 4], ALU.subtract)
                dve.tensor_tensor(squares, stats[:, tiles, 2], stats[:, tiles, 5], ALU.add)
                dve.drain()
                dve.tensor_scalar(mean[:, tiles], total, 0.5, None, ALU.mult)
                dve.scalar_tensor_tensor(half, gap, 0.25, gap, ALU.mult, ALU.mult)
                dve.tensor_scalar(squares, squares, 1.0 / D, LN_EPS, ALU.mult, ALU.add)
                dve.drain()
                dve.tensor_tensor(var[:, tiles], squares, half, ALU.add).then_inc(s_lnv, 1)

            def ln_inverse(n, tiles):
                dve.wait_ge(s_std, n)
                dve.reciprocal(rstd[:, tiles], std[:, tiles]).then_inc(s_ln, 1)
                dve.wait_ge(s_ln, n)

            def normalise(dst, j):
                return dve.tensor_scalar(dst, X[:, ds(j, 1), :].rearrange("p o d -> p (o d)"), mean[:, ds(j, 1)],
                                         rstd[:, ds(j, 1)], ALU.subtract, ALU.mult)

            def norm4(m, tg):
                wait(dve, s_xt_ps, TG * m + tg - 1)
                for i in range(GT):
                    mm = normalise(xn4[:, tg % 2, i, :], GT * tg + i)
                mm.then_inc(s_xn4, 1)

            for tg in range(TG):
                dve.wait_ge(s_x[tg], 16)
                tile_stats(GT * tg, GT)
            ln_variance(ALL)
            ln_inverse(1, ALL)

            def front(b, o):
                for c in range(TB):
                    j = TB * b + c
                    dve.tensor_scalar(xn[:, o, c, :], X[:, ds(j, 1), :].rearrange("p o d -> p (o d)"),
                                      mean[:, ds(j, 1)], rstd[:, ds(j, 1)],
                                      ALU.subtract, ALU.mult).then_inc(s_xn, 1)

            def front_step(b, o, first, last):
                if within(b + 2):
                    dve.wait_ge(s_xn_ps, b + 1)
                    front(b + 2, o)
                dve.wait_ge(s_xpad, b + 1)
                n = KI * (TAPS - 1) * b
                for t in range(TAPS - 1):
                    if t == 0:
                        dve.wait_ge(s_tap0, KI * (b + 1))
                    else:
                        dve.wait_ge(s_tap, n + KI * t)
                    for k in range(KI):
                        dve.scalar_tensor_tensor(conv_o[:, o, k, :], x_pad[:, o, k, t:t + T], conv_w_s[:, k, t:t + 1],
                                                 conv_o[:, o, k, :], ALU.mult, ALU.add).then_inc(s_tap, 1)
                if not first:
                    columns_copy(b - 1, 1 - o)

            def columns_copy(b, o):
                dve.wait_ge(s_xs_t, KI * (b + 1))
                dve.tensor_copy(XST[:, :, ds(b * T, T)], xs_t[:, o, :, :]).then_inc(s_xst, 1)

            front(0, 0)
            front(1, 1)
            dve.wait_ge(s_w_conv, 32)
            pipelined(dve, front_step)
            columns_copy(B - 1, 1)
            v, nabs, u, w, lg, q = tmp
            dve.wait_ge(s_w, W_ALL)
            dve.wait_ge(s_xr, TB * B)
            dve.tensor_tensor(v[:, :, :], XR[:, :, 0, P:XRW], XR[:, :, 1, P:XRW], ALU.add).then_inc(s_dtv, 1)
            dve.wait_ge(s_dtv, 1)
            dve.tensor_tensor(v[:, :, :], v[:, :, :], row_nh[:, 1:2, :].broadcast_to((P, NT, NH)), ALU.add).then_inc(s_dtv, 1)
            dve.wait_ge(s_dtv, 2)
            dve.scalar_tensor_tensor(nabs[:, :, :], v[:, :, :], -1.0, v[:, :, :], ALU.mult, ALU.min).then_inc(s_dtv, 1)
            dve.wait_ge(s_dta, 2)
            dve.tensor_scalar(w[:, :, :], u[:, :, :], 1.0, None, ALU.add).then_inc(s_dtv, 1)
            dve.wait_ge(s_dtv, 4)
            dve.tensor_scalar(q[:, :, :], w[:, :, :], -1.0, 0.0, ALU.add, ALU.is_equal).then_inc(s_dtv, 1)
            dve.wait_ge(s_dtv, 5)
            dve.wait_ge(s_dta, 3)
            dve.scalar_tensor_tensor(w[:, :, :], w[:, :, :], -1.0, q[:, :, :], ALU.add, ALU.add).then_inc(s_dtv, 1)
            dve.tensor_tensor(lg[:, :, :], lg[:, :, :], q[:, :, :], ALU.add).then_inc(s_dtv, 1)
            dve.wait_ge(s_dtv, 7)
            dve.reciprocal(nabs[:, :, :], w[:, :, :]).then_inc(s_dtv, 1)
            dve.tensor_tensor(lg[:, :, :], lg[:, :, :], u[:, :, :], ALU.mult).then_inc(s_dtv, 1)
            dve.wait_ge(s_dtv, 9)
            dve.tensor_tensor(lg[:, :, :], lg[:, :, :], nabs[:, :, :], ALU.mult).then_inc(s_dtv, 1)
            dve.wait_ge(s_dtv, 10)
            dve.scalar_tensor_tensor(DT[:, :, :], v[:, :, :], 0.0, lg[:, :, :], ALU.max, ALU.add).then_inc(s_dtv, 1)
            dve.wait_ge(s_dtv, 11)
            dve.wait_ge(s_dta, 2)
            dve.tensor_tensor(nabs[:, :, :], DT[:, :, :], neg_a[:, :].unsqueeze(1).broadcast_to((P, NT, NH)),
                              ALU.mult).then_inc(s_dtv, 1)

            def decays(b, q):
                dve.wait_ge(s_g_ps, KI * b + q + 1)
                if not (isinstance(b, int) and b == 0):
                    dve.wait_ge(s_wq, 2 * KI * (b - 1) + 2 * (q + 1))
                for r in range(2):
                    dve.tensor_tensor_scan(dec0[:, q, r, :], PS[:, 4 + 3 * q, r * T:(r + 1) * T], ident[:, :], 0.0,
                                           ALU.mult, ALU.add).then_inc(s_dec, 1)
                    dve.tensor_tensor_scan(dec1[:, q, r, :], PS[:, 4 + 3 * q, r * T + P:(r + 1) * T], ident[:, 0:P], 0.0,
                                           ALU.mult, ALU.add).then_inc(s_dec, 1)
                dve.wait_ge(s_dec, 4 * (KI * b + q + 1))
                dve.tensor_tensor(w0[:, q, :, :], dec0[:, q, :, :], PS[:, 2 + 3 * q, :].rearrange("p (r t) -> p r t", r=2),
                                  ALU.mult).then_inc(s_wq, 1)
                dve.tensor_tensor(w1[:, q, :, :], dec1[:, q, :, :],
                                  PS[:, 3 + 3 * q, 0:2 * P].rearrange("p (r t) -> p r t", r=2),
                                  ALU.mult).then_inc(s_wq, 1)

            def y_norm(b, o):
                if not (isinstance(b, int) and b == 0):
                    dve.wait_ge(s_yn, b)
                for c in range(TB):
                    dve.wait_ge(s_y_ps, TB * b + c + 1)
                    for q in range(KI):
                        own = PS[:, 2 + 3 * c, q * T:(q + 1) * T].rearrange("p (r e) -> p r e", r=4)[:, 0:4:3, :]
                        m = dve.tensor_tensor(y[:, c, q * P:(q + 1) * P].rearrange("p (r e) -> p r e", r=2), own,
                                              dx[:, o, c, q * P:(q + 1) * P].rearrange("p (r e) -> p r e", r=2), ALU.add)
                    m.then_inc(s_y, 1)
                for c in range(TB):
                    dve.wait_ge(s_y, TB * b + c + 1)
                    dve.bn_stats(yst[:, c, :], y[:, c, :])
                dve.drain()
                for c in range(TB):
                    dve.bn_aggr(ymv[:, c, :], yst[:, c, :]).then_inc(s_ymv, 1)
                dve.wait_ge(s_ysd, b + 1)
                dve.reciprocal(yrs[:, :], ysd[:, :]).then_inc(s_yrs, 1)
                dve.wait_ge(s_yrs, b + 1)
                wait(dve, s_yw, b)
                for c in range(TB):
                    m = dve.tensor_scalar(yn[:, c, :], y[:, c, :], ymv[:, c, 0:1], yrs[:, c:c + 1], ALU.subtract, ALU.mult)
                m.then_inc(s_yn, 1)

            def residual(b):
                dve.wait_ge(s_o_ps, b + 1)
                rows = X[:, ds(TB * b, TB), :]
                dve.tensor_tensor(rows, PS[:, 1, 0:T].rearrange("p (c d) -> p c d", c=TB), rows, ALU.add).then_inc(s_o, 1)

            def scan_step(b, o, first, last):
                decays(b, 0)
                if not (isinstance(b, int) and b < 2):
                    residual(b - 2)
                decays(b, 1)
                if last:
                    ln_variance(EARLY)
                y_norm(b, o)
                if not (isinstance(b, int) and b < 2):
                    dve.wait_ge(s_o, b - 1)
                    tile_stats(TB * (b - 2), TB)

            pipelined(dve, scan_step)
            ln_inverse(LN_MOE[0], EARLY)
            residual(B - 2)
            norm4(0, 0)
            norm4(0, 1)
            dve.wait_ge(s_o, B - 1)
            tile_stats(TB * (B - 2), TB)
            residual(B - 1)
            end_phase(dve, 1)

            def best(m):
                for j in range(NT):
                    dve.max(top[:, j, :], logits[:, j, :])
                dve.drain()
                dve.tensor_tensor(top_g[:, 0, :], top[:, :, 1], top[:, :, 0], ALU.subtract).then_inc(s_top, 1)

            def which(m):
                for j in range(NT):
                    dve.max_index(top_i[:, j, :], top[:, j, :], logits[:, j, :])
                dve.wait_ge(s_e, m + 1)
                dve.tensor_scalar(top_g[:, 2, :], top_g[:, 1, :], 1.0, None, ALU.add)
                dve.drain()
                dve.tensor_copy(top_if[:, :, :], top_i[:, :, 0:2])
                dve.reciprocal(top_g[:, 3, :], top_g[:, 2, :])
                dve.drain()
                dve.tensor_tensor(top_g[:, 2, :], top_g[:, 1, :], top_g[:, 3, :], ALU.mult)
                for i in range(2):
                    dve.tensor_tensor(pick[:, i, :, :], iota[:, :].unsqueeze(1).broadcast_to((P, NT, NE)),
                                      top_if[:, :, i:i + 1].broadcast_to((P, NT, NE)), ALU.is_equal)
                dve.drain()
                for i in range(2):
                    dve.tensor_tensor(pick[:, i, :, :], pick[:, i, :, :],
                                      top_g[:, 3 - i, :].unsqueeze(2).broadcast_to((P, NT, NE)), ALU.mult)
                dve.drain()
                dve.tensor_tensor(gates[:, :, :].rearrange("p e j -> p j e"), pick[:, 0, :, :], pick[:, 1, :, :],
                                  ALU.add).then_inc(s_gates, 1)

            def gates_columns(m):
                dve.wait_ge(s_gates_ps, m + 1)
                dve.tensor_copy(gates_t[:, :], PS[:, 7, 0:P]).then_inc(s_gates_t, 1)

            def moe_dve(m, phase):
                def low(n, tg):
                    o = tg % 2
                    if not (isinstance(n, int) and n < 2):
                        dve.wait_ge(s_down, n - 1)
                    for h in range(2):
                        dve.wait_ge(s_hi, 2 * n + h + 1)
                        dve.tensor_tensor(h_lo[:, o, h, :], h_f[:, o, h, :], h_hi[:, o, h, :].bitcast(F32),
                                          ALU.subtract).then_inc(s_lo, 1)

                def high_part(tg):
                    dve.wait_ge(s_xt, TG * m + tg + 1)
                    cols = slice(GN * tg, GN * (tg + 1))
                    dve.tensor_copy(XH[:, cols], xt4[:, tg % 2, :]).then_inc(s_xl, 1)

                def low_part(tg):
                    dve.wait_ge(s_xl, 2 * (TG * m + tg) + 1)
                    cols = slice(GN * tg, GN * (tg + 1))
                    dve.tensor_tensor(XL[:, cols], xt4[:, tg % 2, :], XH[:, cols].bitcast(F32), ALU.subtract).then_inc(s_xl, 1)

                def logits_copy(tg):
                    dve.wait_ge(s_lg_ps, TG * m + tg + 1)
                    dve.tensor_copy(logits[:, GT * tg:GT * (tg + 1), :].rearrange("p j e -> p (j e)"),
                                    PS[:, 7 - 3 * (tg % 2), 0:GT * NE]).then_inc(s_lg, 1)

                high_part(0)
                dve.wait_ge(s_res_a if m else s_o, B)
                tile_stats(TB * (B - 1), TB)
                low_part(0)
                ln_variance(LATE)
                high_part(1)
                low_part(1)
                ln_inverse(LN_MOE[m] + 1, LATE)
                norm4(m, 2)
                norm4(m, 3)
                logits_copy(0)
                logits_copy(1)
                high_part(2)
                low_part(2)
                low(UNITS * m, 0)
                logits_copy(2)
                high_part(3)
                low_part(3)
                logits_copy(3)
                dve.wait_ge(s_lg, TG * (m + 1))

                def gate(k, tg, o=None, i=None):
                    n = UNITS * m + TG * k + tg
                    dve.wait_ge(s_down, n + 1)
                    cols = slice(tg * GN, (tg + 1) * GN)
                    if not (isinstance(n, int) and n < 2):
                        dve.wait_ge(s_acc, n - 1)
                    if o is None:
                        dve.tensor_copy(gy[:, tg % 2, :], PS[:, 4 + tg % 2, :]).then_inc(s_gated, 1)
                        return
                    if tg == 0:
                        dve.wait_ge(s_gb[o], 16 * (NE // 2 * m + i + 1))
                    dve.tensor_tensor(gy[:, tg % 2, :], gates_b[:, o, cols], PS[:, 4 + tg % 2, :], ALU.mult).then_inc(s_gated, 1)

                def residual(tg):
                    dve.wait_ge(s_acc_ps, TG * m + tg + 1)
                    rows = X[:, GT * tg:GT * (tg + 1), :]
                    dve.tensor_tensor(rows, PS[:, 6 + tg % 2, :].rearrange("p (i d) -> p i d", i=GT), rows,
                                      ALU.add).then_inc(s_res, 1)

                def next_stats(tg):
                    if m == 0:
                        dve.wait_ge(s_res, TG * m + tg + 1)
                        tile_stats(GT * tg, GT)

                best(m)
                low(UNITS * m + 1, 1)
                gate(0, 0)
                which(m)
                low(UNITS * m + 2, 2)
                gate(0, 1)
                gates_columns(m)
                low(UNITS * m + 3, 3)
                gate(0, 2)
                low(UNITS * m + TG, 0)
                gate(0, TG - 1)
                with dve.Fori(0, NE // 2 - 1) as i:
                    for o in range(2):
                        k = 2 * i + 1 + o
                        for tg in range(TG):
                            low(UNITS * m + TG * k + tg + 1, (tg + 1) % TG)
                            gate(k, tg, o, i)
                for o in range(2):
                    k = NE - 1 + o
                    for tg in range(TG):
                        if k < NE or tg < TG - 1:
                            low(UNITS * m + TG * k + tg + 1, (tg + 1) % TG)
                        gate(k, tg, o, NE // 2 - 1)
                        if k == NE and tg == TG - 1:
                            dve.wait_ge(s_gated, UNITS * (m + 1))
                            dve.wait_ge(s_acc, UNITS * (m + 1) - 1)
                            part = acc[:, tg * GN:]
                            dve.tensor_tensor(part, part, gy[:, tg % 2, :], ALU.add).then_inc(s_acc, 1)
                        if k == NE and tg == 2:
                            residual(0)
                            residual(1)
                residual(2)
                next_stats(0)
                next_stats(1)
                residual(3)
                end_phase(dve, phase)
                for tg in range(2, TG):
                    next_stats(tg)

            def attn_dve():
                ln_variance(ALL)
                dve.wait_ge(s_aw, 16 * 10)
                dve.wait_ge(s_ac, 11)
                dve.wait_ge(s_aw_ps, 1)
                dve.tensor_copy(small[:, 0:2 * HD], PS[0:HD, 7, 0:2 * HD]).then_inc(s_aw_c, 1)
                dve.scalar_tensor_tensor(small[:, 3 * HD:4 * HD], PS[0:HD, 7, 3 * HD:4 * HD], HD ** -0.5,
                                         row_qk[0:HD, 0, :], ALU.mult, ALU.mult).then_inc(s_aw_c, 1)
                dve.tensor_copy(av[:, :], PS[0:HD, 7, 4 * HD:5 * HD]).then_inc(s_aw_c, 1)
                dve.wait_ge(s_aw_ps, 2)
                dve.tensor_copy(small[:, 2 * HD:3 * HD], PS[0:HD, 6, 0:HD]).then_inc(s_aw_c, 1)
                dve.scalar_tensor_tensor(row_qk[:, 2, :], row_qk[:, 0, :], HD ** -0.5, row_qk[:, 1, :], ALU.mult,
                                         ALU.mult).then_inc(s_wa, 1)
                dve.wait_ge(s_aw_ps, 3)
                dve.tensor_copy(wa_rep[:, :], PS[:, 7, 0:NSEC * HD])
                dve.drain()
                ln_inverse(4, ALL)

                def front(b, o):
                    wait(dve, s_xa_ps, b - 1)
                    for c in range(TB):
                        normalise(xa[:, o, c, :], TB * b + c).then_inc(s_xa, 1)

                def square_sums(b, o):
                    for c in range(TB):
                        dve.wait_ge(s_sq, TB * b + c + 1)
                        dve.tensor_reduce(ss[:, ds(TB * b + c, 1), :].rearrange("p o h -> p (o h)"),
                                          sq[:, o, c, :].rearrange("p (h e) -> p h e", e=HD), AX.X, ALU.add).then_inc(s_ss, 1)

                def front_step(b, o, first, last):
                    if not last:
                        front(b + 1, 1 - o)
                    if not first:
                        square_sums(b - 1, 1 - o)
                    if isinstance(b, int) and b == 1:
                        inverses(0)

                def inverses(part):
                    tiles = (slice(0, TB), slice(TB, NT))[part]
                    dve.wait_ge(s_ss, (TB, NT)[part])
                    dve.tensor_scalar(ss[:, tiles, :], ss[:, tiles, :], 1.0 / HD, RMS_EPS, ALU.mult, ALU.add).then_inc(s_ms, 1)
                    dve.wait_ge(s_rs, part + 1)
                    dve.reciprocal(rr[:, tiles, :], rr[:, tiles, :]).then_inc(s_rr, 1)

                front(0, 0)
                for i in range(NSEC):
                    dve.tensor_tensor(w_all[:, i, :, :], wa_rep[:, i * HD:(i + 1) * HD].unsqueeze(1).broadcast_to((P, H, HD)),
                                      head_of[:, :].unsqueeze(2).broadcast_to((P, H, HD)), ALU.mult).then_inc(s_wa, 1)
                pipelined(dve, front_step)
                square_sums(B - 1, 1)
                inverses(1)

                def flat(t):
                    return t.rearrange("p c (h e) -> p (c h) e", h=H)

                def maxima(b, g_):
                    for c in range(TB):
                        i = TB * g_ + c
                        dve.wait_ge(s_p1, 8 * b + i + 1)
                        scores = PS[:, 4 + 2 * (i % 2):6 + 2 * (i % 2), :].rearrange("p k (j t) -> p (k j) t", j=2)
                        dve.tensor_reduce(neg_max[:, c, 4 * g_:4 * g_ + 4], scores[:, :, 0:(c + 1) * P], AX.X, ALU.max,
                                          negate=True).then_inc(s_max, 1)

                def place(b, o, half):
                    dve.wait_ge(s_max, 8 * b + 4 * (half + 1))
                    heads = slice(8 * half, 8 * (half + 1))
                    nm = neg_max[:, :, heads]
                    nm_hi, nm_lo = (q_pad[:, o, :, heads, 3 * HD + a] for a in range(2))
                    dve.tensor_copy(nm_hi.bitcast(F32R), nm).then_inc(s_nm, 1)
                    dve.wait_ge(s_nm, 4 * b + 2 * half + 1)
                    dve.tensor_tensor(nm_lo.bitcast(F32R), nm, nm_hi, ALU.subtract).then_inc(s_nm, 1)

                def finish(b):
                    dve.wait_ge(s_or_ps, b + 1)
                    rows = PS[:, 2:4, :].rearrange("p c (h s) -> p c h s", s=SLOT)
                    dve.reciprocal(den[:, :, :], rows[:, :, :, HD]).then_inc(s_den, 1)
                    dve.wait_ge(s_den, b + 1)
                    dve.tensor_tensor(flat(o_r[:, :, :]), rows[:, :, :, 0:HD].rearrange("p c h e -> p (c h) e"),
                                      den[:, :, :].rearrange("p c (h o) -> p (c h) o", o=1).broadcast_to((P, TB * H, HD)),
                                      ALU.mult).then_inc(s_or, 1)
                    dve.wait_ge(s_or, b + 1)
                    rows = X[:, ds(TB * b, TB), :]
                    dve.tensor_tensor(rows, rows, o_r[:, :, :], ALU.add).then_inc(s_res_a, 1)

                def next_stats(b):
                    dve.wait_ge(s_res_a, b + 1)
                    tile_stats(TB * b, TB)

                def queries(b):
                    dve.wait_ge(s_qt_ps, b + 1)
                    dve.tensor_copy(q_t[:, 0, 2:4, :], PS[:, 3, :].rearrange("p (g t) -> p g t", g=2)).then_inc(s_qt[1], 1)

                def step(b, o, first, last):
                    wait(dve, s_nm, 4 * b)
                    maxima(b, 0)
                    maxima(b, 1)
                    place(b, o, 0)
                    maxima(b, 2)
                    maxima(b, 3)
                    place(b, o, 1)
                    dve.wait_ge(s_qf_ps, 2 * b + 2)
                    dve.tensor_copy(q_t[:, 1, 2:4, :], PS[:, 3, :].rearrange("p (g t) -> p g t", g=2)).then_inc(s_qf[1], 1)
                    if not first:
                        wait(dve, s_res_a, b - 1)
                        finish(b - 1)
                        next_stats(b - 1)
                    if not last:
                        queries(b + 1)
                    if last:
                        ln_variance(EARLY)

                queries(0)
                pipelined(dve, step)
                ln_inverse(LN_MOE[1], EARLY)
                norm4(1, 0)
                norm4(1, 1)
                finish(B - 1)
                end_phase(dve, 3)

            moe_dve(0, 2)
            attn_dve()
            moe_dve(1, 4)


_INPUTS = ("x", "w_in", "conv_w", "conv_b", "a_log", "dt_w", "dt_b", "b_w", "c_w", "d_skip", "ln_w", "ln_b", "w_out",
           "w_dq", "w_uq_t", "w_dkv", "w_ukv_t", "w_qr", "w_kr", "w_o_t", "qn_w", "kn_w", "moe_w1", "moe_w2", "gate_w")


def kernel(**inputs):
    import numpy as np
    import concourse.bacc as bacc
    from concourse.bass_utils import run_bass_kernel_spmd as run

    i = {k: np.asarray(v) for k, v in inputs.items()}
    a, m, f = ({k[len(p):]: v for k, v in i.items() if k.startswith(p)} for p in ("L0_attn_a_", "L0_attn_b_", "L0_ffn_"))
    x = a["hidden_states"]
    by_chunk = lambda w: w.T.reshape(2, 128, -1).transpose(1, 0, 2)
    arrays = dict(
        x=x.reshape(-1, x.shape[-1]), w_in=a["in_proj_w"].T,
        conv_w=a["conv_w"].reshape(2, 128, -1).transpose(1, 0, 2), conv_b=a["conv_b"].reshape(2, 128).T,
        a_log=a["A_log"][None], dt_w=by_chunk(a["dt_w"]), dt_b=a["dt_b"][None],
        b_w=by_chunk(a["B_w"]), c_w=by_chunk(a["C_w"]), d_skip=a["D"][None], ln_w=a["ln_w"][None], ln_b=a["ln_b"][None],
        w_out=a["out_proj_w"].T.reshape(2, 128, -1),
        w_dq=m["W_DQ"], w_uq_t=m["W_UQ"].T, w_dkv=m["W_DKV"], w_ukv_t=m["W_UKV"].T, w_qr=m["W_QR"], w_kr=m["W_KR"],
        w_o_t=m["W_O"].T, qn_w=m["q_norm_w"][None], kn_w=m["k_norm_w"][None],
        moe_w1=np.concatenate([f["shared_w1"][None], f["experts_w1"]]).transpose(0, 2, 1),
        moe_w2=np.concatenate([f["shared_w2"][None], f["experts_w2"]]).transpose(0, 2, 1).reshape(9, 4, 128, 128).transpose(0, 2, 1, 3),
        gate_w=f["gate_w"].T,
    )
    arrays = {k: np.ascontiguousarray(arrays[k]) for k in _INPUTS}
    nc = bacc.Bacc("TRN2", target_bir_lowering=False, num_devices=1)
    args = [nc.dram_tensor(k, arrays[k].shape, mybir.dt.from_np(arrays[k].dtype), kind="ExternalInput").ap() for k in _INPUTS]
    o = nc.dram_tensor("out", arrays["x"].shape, F32, kind="ExternalOutput").ap()
    hybrid_kernel(nc, *args, o)
    r = run(nc, [arrays], core_ids=[0])
    return np.asarray(r.results[0]["out"]).reshape(x.shape)
```
